# Optimizing a Trainium2 kernel written in Bass

```python
import numpy as np
import jax
import jax.numpy as jnp

def _softmax(x, axis=-1):
    return jax.nn.softmax(x, axis=axis)

def _gelu(x):
    return jax.nn.gelu(x, approximate=True)

def _silu(x):
    return jax.nn.silu(x)

def _sigmoid(x):
    return jax.nn.sigmoid(x)

def _layernorm(x, axis=-1, eps=1e-05):
    m = jnp.mean(x, axis=axis, keepdims=True)
    v = jnp.var(x, axis=axis, keepdims=True)
    return (x - m) / jnp.sqrt(v + eps)

def _scatter_add(tgt, idx, src, axis=0):
    return tgt.at[idx].add(src)

def _segment_sum(src, seg, n):
    return jax.ops.segment_sum(src, seg, n)
kernel_name = 'mk_adj_seq_d1_adj_r2_db3cd1'

def setup_inputs(seed: int=0):
    np.random.seed(seed)
    _w = jnp.asarray

    def _rec_inputs():
        import jax
        import jax.numpy as jnp
        _gk = jax.random.key(seed)
        x = -0.0005207 + 1.001 * jax.random.normal(jax.random.fold_in(_gk, 1), (4096, 256), jnp.float32)
        _a = jax.random.bernoulli(jax.random.fold_in(_gk, 2), 0.00195312, (4096, 4096))
        adj = _a.astype(jnp.int32)
        return (x, adj)
    x, adj = _rec_inputs()

    def _L0_gnn_setup():
        import jax, jax.numpy as jnp
        import numpy as np
        D_MODEL = 256
        N_HEADS = 8
        D_K = D_MODEL // N_HEADS
        D_FF = 1024
        N = 2048
        EPS = 1e-05

        def _layer_norm(x, g, b):
            mu = jnp.mean(x, axis=-1, keepdims=True)
            var = jnp.mean(jnp.square(x - mu), axis=-1, keepdims=True)
            return (x - mu) * jax.lax.rsqrt(var + EPS) * g + b
        key = jax.random.key(seed)
        ks = jax.random.split(key, 16)
        s = 1.0 / np.sqrt(D_MODEL)
        sf = 1.0 / np.sqrt(D_FF)
        inp = {'h': jax.random.normal(ks[0], (N, D_MODEL), dtype=jnp.float32), 'adj': jax.random.randint(ks[1], (N, N), 0, 2, dtype=jnp.int32), 'Wq': jax.random.uniform(ks[2], (D_MODEL, D_MODEL), jnp.float32, -s, s), 'bq': jnp.zeros((D_MODEL,), jnp.float32), 'Wk': jax.random.uniform(ks[3], (D_MODEL, D_MODEL), jnp.float32, -s, s), 'bk': jnp.zeros((D_MODEL,), jnp.float32), 'Wv': jax.random.uniform(ks[4], (D_MODEL, D_MODEL), jnp.float32, -s, s), 'bv': jnp.zeros((D_MODEL,), jnp.float32), 'Wo': jax.random.uniform(ks[5], (D_MODEL, D_MODEL), jnp.float32, -s, s), 'bo': jnp.zeros((D_MODEL,), jnp.float32), 'W1': jax.random.uniform(ks[6], (D_FF, D_MODEL), jnp.float32, -s, s), 'b1': jnp.zeros((D_FF,), jnp.float32), 'W2': jax.random.uniform(ks[7], (D_MODEL, D_FF), jnp.float32, -sf, sf), 'b2': jnp.zeros((D_MODEL,), jnp.float32), 'ln1_g': jnp.ones((D_MODEL,), jnp.float32), 'ln1_b': jnp.zeros((D_MODEL,), jnp.float32), 'ln2_g': jnp.ones((D_MODEL,), jnp.float32), 'ln2_b': jnp.zeros((D_MODEL,), jnp.float32)}
        return inp
    _L0_gnn_all = _L0_gnn_setup()
    _L0_gnn_in = {k: v for k, v in _L0_gnn_all.items() if k in ('Wq', 'bq', 'Wk', 'bk', 'Wv', 'bv', 'Wo', 'bo', 'W1', 'b1', 'W2', 'b2', 'ln1_g', 'ln1_b', 'ln2_g', 'ln2_b')}
    del _L0_gnn_all
    return {'x': x, 'adj': adj, 'L0_gnn_Wq': _L0_gnn_in['Wq'], 'L0_gnn_bq': _L0_gnn_in['bq'], 'L0_gnn_Wk': _L0_gnn_in['Wk'], 'L0_gnn_bk': _L0_gnn_in['bk'], 'L0_gnn_Wv': _L0_gnn_in['Wv'], 'L0_gnn_bv': _L0_gnn_in['bv'], 'L0_gnn_Wo': _L0_gnn_in['Wo'], 'L0_gnn_bo': _L0_gnn_in['bo'], 'L0_gnn_W1': _L0_gnn_in['W1'], 'L0_gnn_b1': _L0_gnn_in['b1'], 'L0_gnn_W2': _L0_gnn_in['W2'], 'L0_gnn_b2': _L0_gnn_in['b2'], 'L0_gnn_ln1_g': _L0_gnn_in['ln1_g'], 'L0_gnn_ln1_b': _L0_gnn_in['ln1_b'], 'L0_gnn_ln2_g': _L0_gnn_in['ln2_g'], 'L0_gnn_ln2_b': _L0_gnn_in['ln2_b']}

def reference(x, adj, L0_gnn_Wq, L0_gnn_bq, L0_gnn_Wk, L0_gnn_bk, L0_gnn_Wv, L0_gnn_bv, L0_gnn_Wo, L0_gnn_bo, L0_gnn_W1, L0_gnn_b1, L0_gnn_W2, L0_gnn_b2, L0_gnn_ln1_g, L0_gnn_ln1_b, L0_gnn_ln2_g, L0_gnn_ln2_b):
    import jax
    import jax.numpy as jnp

    def _L0_gnn_ref(h, adj, Wq, bq, Wk, bk, Wv, bv, Wo, bo, W1, b1, W2, b2, ln1_g, ln1_b, ln2_g, ln2_b):
        import jax, jax.numpy as jnp
        import numpy as np
        D_MODEL = 256
        N_HEADS = 8
        D_K = D_MODEL // N_HEADS
        D_FF = 1024
        N = 2048
        EPS = 1e-05

        def _layer_norm(x, g, b):
            mu = jnp.mean(x, axis=-1, keepdims=True)
            var = jnp.mean(jnp.square(x - mu), axis=-1, keepdims=True)
            return (x - mu) * jax.lax.rsqrt(var + EPS) * g + b
        n = h.shape[0]
        mask = adj.astype(jnp.float32) + jnp.eye(n, dtype=jnp.float32)
        q = (h @ Wq.T + bq).reshape(n, N_HEADS, D_K)
        k = (h @ Wk.T + bk).reshape(n, N_HEADS, D_K)
        v = (h @ Wv.T + bv).reshape(n, N_HEADS, D_K)
        scores = jnp.einsum('nhd,mhd->hnm', q, k) / jnp.sqrt(jnp.float32(D_K))
        scores = jnp.where(mask[None, :, :] == 0, jnp.float32(-1000000000.0), scores)
        attn = jax.nn.softmax(scores, axis=-1)
        ctx = jnp.einsum('hnm,mhd->nhd', attn, v).reshape(n, D_MODEL)
        attn_out = ctx @ Wo.T + bo
        h1 = _layer_norm(h + attn_out, ln1_g, ln1_b)
        ff = jax.nn.relu(h1 @ W1.T + b1) @ W2.T + b2
        h2 = _layer_norm(h1 + ff, ln2_g, ln2_b)
        return h2
    x = _L0_gnn_ref(x, adj, L0_gnn_Wq, L0_gnn_bq, L0_gnn_Wk, L0_gnn_bk, L0_gnn_Wv, L0_gnn_bv, L0_gnn_Wo, L0_gnn_bo, L0_gnn_W1, L0_gnn_b1, L0_gnn_W2, L0_gnn_b2, L0_gnn_ln1_g, L0_gnn_ln1_b, L0_gnn_ln2_g, L0_gnn_ln2_b)
    return x

_drawn_inputs = setup_inputs


def setup_inputs(seed=0):
    import zlib

    import numpy as np

    out = dict(_drawn_inputs(seed))
    spreads = {'L0_gnn_bq': (0.0, 0.8),
     'L0_gnn_bk': (0.0, 0.8),
     'L0_gnn_bv': (0.0, 0.1),
     'L0_gnn_bo': (0.0, 0.1),
     'L0_gnn_b1': (0.0, 0.1),
     'L0_gnn_b2': (0.0, 0.1),
     'L0_gnn_ln1_g': (1.0, 0.2),
     'L0_gnn_ln1_b': (0.0, 0.1),
     'L0_gnn_ln2_g': (1.0, 0.2),
     'L0_gnn_ln2_b': (0.0, 0.1)}
    factors = {}
    for name, (base, spread) in spreads.items():
        noise = np.random.default_rng([zlib.crc32(name.encode()), seed]).standard_normal(out[name].shape)
        drawn = base * np.exp(spread * noise) if base else spread * noise
        out[name] = jnp.asarray(drawn.astype(out[name].dtype))
    for name, factor in factors.items():
        out[name] = (out[name] * factor).astype(out[name].dtype)
    return out
```

```python
import concourse.bass as bass
from concourse import mybir
from contextlib import ExitStack


def build_gnn_layer(nc, x, adj, Wq, bq, Wk, bk, Wv, bv, Wo, bo, W1, b1, W2, b2,
                    ln1_g, ln1_b, ln2_g, ln2_b, out):
    fp32, fp32r, bf16, i32 = (mybir.dt.float32, mybir.dt.float32r, mybir.dt.bfloat16, mybir.dt.int32)
    ALU, ACT, AX = mybir.AluOpType, mybir.ActivationFunctionType, mybir.AxisListType
    ds = bass.ds

    N, D = x.shape
    FF = W1.shape[0]
    P = 128
    BANK = 512
    HEADS, DK = 8, 32
    GROUP = P // DK
    GROUPS = HEADS // GROUP
    HALVES = 4
    KB = D // P
    FB = FF // P
    TILES = N // P
    SUB = BANK // P
    BLOCKS = N // BANK
    SCALE = float(DK) ** -0.5
    MASKED = -1.0e9 / SCALE
    LOWEST = -3.0e38
    EPS = 1e-5

    k_halves = nc.dram_tensor("k_halves", (HALVES, D, N), fp32, kind="Internal").ap()
    q_halves = nc.dram_tensor("q_halves", (HALVES, D, N), fp32, kind="Internal").ap()
    ctx_dram = nc.dram_tensor("ctx_rows", (N, D), fp32, kind="Internal").ap()

    def expected(eng):
        register = eng.alloc_register()
        eng.reg_mov(register, 0)
        return register

    def wait_then_add(eng, semaphore, register, step):
        eng.wait_ge(semaphore, register)
        eng.reg_alu(register, register, step, ALU.add)

    def allocators(stack):
        def sb(name, shape, dt=fp32):
            return stack.enter_context(nc.sbuf_tensor(name, shape, dt))

        def bank(name):
            return stack.enter_context(nc.psum_tensor(name, [P, BANK], fp32))

        def sem(name):
            return stack.enter_context(nc.semaphore(name))
        return sb, bank, sem

    def token_block(a, b):
        return a[ds(b * BANK, BANK), :].rearrange("(s p) d -> p s d", p=P)

    whole = ExitStack()
    with whole:
        sb, bank, sem = allocators(whole)
        ident = sb("ident", [P, P])
        v_sb = sb("v_sb", [P, TILES, D])

        with ExitStack() as stage:
            sb, bank, sem = allocators(stage)
            w_rows = [sb(f"w_rows{w}", [P, KB, D]) for w in range(3)]
            w_cols = [sb(f"w_cols{w}", [P, KB, D]) for w in range(3)]
            bias_k = sb("bias_k", [P, KB])
            bias_q = sb("bias_q", [P, KB])
            bias_v = sb("bias_v", [P, 2, D])
            x_rows = [sb(f"x_rows{i}", [P, SUB, D]) for i in range(2)]
            x_cols = [sb(f"x_cols{i}", [P, KB, BANK]) for i in range(2)]
            high = [[sb(f"high{i}_{o}", [P, BANK], fp32r) for o in range(4)] for i in range(2)]
            low = [[sb(f"low{i}_{o}", [P, BANK], fp32r) for o in range(4)] for i in range(2)]
            w_ps = [bank(f"w_ps{i}") for i in range(2)]
            x_ps = [bank(f"x_ps{i}") for i in range(2)]
            qk_ps = [bank(f"qk_ps{i}") for i in range(2)]
            v_ps = [bank(f"v_ps{i}") for i in range(2)]

            w_in = sem("w_in")
            bias_in = sem("bias_in")
            ident_zeroed = sem("ident_zeroed")
            ident_ready = sem("ident_ready")
            w_turned = sem("w_turned")
            w_copied = sem("w_copied")
            x_in = [sem(f"x_in{i}") for i in range(2)]
            x_turned = sem("x_turned")
            x_copied = sem("x_copied")
            qk_done = sem("qk_done")
            high_ready = sem("high_ready")
            low_ready = sem("low_ready")
            halves_stored = [sem(f"halves_stored{i}") for i in range(2)]
            v_done = sem("v_done")
            v_ready = sem("v_ready")
            PAIRS = BLOCKS // 2
            STORES = 4 * HALVES

            def pairwise(eng, pair):
                pair(0)
                with eng.Fori(1, PAIRS) as i:
                    pair(i)

            def wait_reused(eng, semaphore, value):
                if not isinstance(value, int) or value > 0:
                    eng.wait_ge(semaphore, value)

            block = stage.enter_context(nc.Block())

            @block.gpsimd
            def _(pool):
                nc.gpsimd.memset(ident[:, :], 0.0).then_inc(ident_zeroed, 1)
                pool.wait_ge(ident_zeroed, 1)
                nc.gpsimd.affine_select(out=ident[:, :], in_=ident[:, :], compare_op=ALU.not_equal,
                                        fill=1.0, base=0, pattern=[[-1, P]],
                                        channel_multiplier=1).then_inc(ident_ready, 1)

            @block.sync
            def _(sp):
                for rows, w in zip(w_rows, (Wk, Wq, Wv)):
                    sp.dma_start(rows[:, :, :], w.rearrange("(f p) d -> p f d", p=P)).then_inc(w_in, 16)
                with nc.allow_non_contiguous_dma(reason="two columns of biases"):
                    sp.dma_start(bias_k[:, :], bk.rearrange("(f p) -> p f", p=P)).then_inc(bias_in, 16)
                    sp.dma_start(bias_q[:, :], bq.rearrange("(f p) -> p f", p=P)).then_inc(bias_in, 16)
                for s in range(2):
                    sp.dma_start(bias_v[:, s, :], bv.partition_broadcast(P)).then_inc(bias_in, 16)
                high_next, low_next = expected(sp), expected(sp)

                def pair(i):
                    first = isinstance(i, int)
                    for par in range(2):
                        wait_reused(sp, x_turned, 4 * i + 2 * par - 2 if not first else 0)
                        sp.dma_start(x_rows[par][:, :, :], token_block(x, 2 * i + par)).then_inc(x_in[par], 16)
                    for par in range(2):
                        cols = ds((2 * i + par) * BANK, BANK)
                        for o in range(4):
                            n = 8 * i + 4 * par + o
                            dst = (k_halves, q_halves)[o // KB]
                            rows = slice((o % KB) * P, (o % KB + 1) * P)
                            high_at = ((0, 2), (0, 1))[o // KB]
                            low_at = ((1, 3), (2, 3))[o // KB]
                            if first:
                                sp.wait_ge(high_ready, n + 1)
                            elif o == 0:
                                wait_then_add(sp, high_ready, high_next, 1)
                            else:
                                sp.wait_ge(high_ready, high_next)
                            for r in high_at:
                                sp.dma_start(dst[r, rows, cols],
                                             high[par][o][:, :].bitcast(fp32)).then_inc(halves_stored[par], 16)
                            if first:
                                sp.wait_ge(low_ready, n + 1)
                            else:
                                if o > 0:
                                    sp.reg_alu(high_next, high_next, 1, ALU.add)
                                sp.wait_ge(low_ready, low_next)
                            for r in low_at:
                                sp.dma_start(dst[r, rows, cols],
                                             low[par][o][:, :].bitcast(fp32)).then_inc(halves_stored[par], 16)
                            if not first:
                                sp.reg_alu(low_next, low_next, 1, ALU.add)

                pair(0)
                sp.reg_mov(high_next, 9)
                sp.reg_mov(low_next, 9)
                with sp.Fori(1, PAIRS) as i:
                    pair(i)
                for par in range(2):
                    sp.wait_ge(halves_stored[par], PAIRS * STORES * 16)

            @block.tensor
            def _(pe):
                pe.wait_ge(ident_ready, 1)
                pe.wait_ge(w_in, 48)
                for w in range(3):
                    if w == 2:
                        pe.wait_ge(w_copied, 1)
                    for c in range(KB):
                        for f in range(KB):
                            last = nc.tensor.transpose(w_ps[w % 2][:, c * D + f * P:c * D + (f + 1) * P],
                                                       w_rows[w][:, f, c * P:(c + 1) * P], ident[:, :])
                    last.then_inc(w_turned, 1)
                pe.wait_ge(w_copied, 3)

                def pair(i):
                    for par in range(2):
                        pe.wait_ge(x_in[par], 16 * i + 16)
                        wait_reused(pe, x_copied, 4 * i + 2 * par)
                        for c in range(KB):
                            for s in range(SUB):
                                last = nc.tensor.transpose(x_ps[c][:, s * P:(s + 1) * P],
                                                           x_rows[par][:, s, c * P:(c + 1) * P], ident[:, :])
                            last.then_inc(x_turned, 1)
                        pe.wait_ge(x_copied, 4 * i + 2 * par + 2)
                        for o in range(4):
                            w, f = o // KB, o % KB
                            n = 8 * i + 4 * par + o
                            wait_reused(pe, low_ready, n - 1)
                            for c in range(KB):
                                last = nc.tensor.matmul(qk_ps[o % 2][:, :], w_cols[w][:, c, f * P:(f + 1) * P],
                                                        x_cols[par][:, c, :], start=(c == 0), stop=(c == KB - 1))
                            last.then_inc(qk_done, 1)
                        for k in range(2):
                            wait_reused(pe, v_ready, 4 * i + 2 * par)
                            for s in range(2):
                                for c in range(KB):
                                    last = nc.tensor.matmul(
                                        v_ps[k][:, s * D:(s + 1) * D],
                                        x_cols[par][:, c, (2 * k + s) * P:(2 * k + s + 1) * P],
                                        w_cols[2][:, c, :], start=(c == 0), stop=(c == KB - 1))
                            last.then_inc(v_done, 1)

                pairwise(pe, pair)

            @block.scalar
            def _(act):
                for w in range(3):
                    act.wait_ge(w_turned, w + 1)
                    nc.scalar.activation(w_cols[w][:, :, :].rearrange("p c n -> p (c n)"), w_ps[w % 2][:, :],
                                         ACT.Copy).then_inc(w_copied, 1)
                act.wait_ge(bias_in, 64)
                def pair(i):
                    for par in range(2):
                        wait_reused(act, v_done, 4 * i + 2 * par - 2)
                        for c in range(KB):
                            act.wait_ge(x_turned, 4 * i + 2 * par + c + 1)
                            nc.scalar.activation(x_cols[par][:, c, :], x_ps[c][:, :], ACT.Copy).then_inc(x_copied, 1)
                        wait_reused(act, halves_stored[par], 16 * STORES * i)
                        for o in range(4):
                            bias = (bias_k, bias_q)[o // KB]
                            act.wait_ge(qk_done, 8 * i + 4 * par + o + 1)
                            nc.scalar.activation(high[par][o][:, :], qk_ps[o % 2][:, :], ACT.Identity,
                                                 bias=bias[:, o % KB:o % KB + 1]).then_inc(high_ready, 1)

                pairwise(act, pair)

            @block.vector
            def _(dve):
                dve.wait_ge(bias_in, 64)
                def pair(i):
                    for par in range(2):
                        wait_reused(dve, halves_stored[par], 16 * STORES * i)
                        for o in range(4):
                            bias = (bias_k, bias_q)[o // KB]
                            dve.wait_ge(high_ready, 8 * i + 4 * par + o + 1)
                            nc.vector.scalar_tensor_tensor(
                                out=low[par][o][:, :], in0=qk_ps[o % 2][:, :], scalar=bias[:, o % KB:o % KB + 1],
                                in1=high[par][o][:, :].bitcast(fp32), op0=ALU.add,
                                op1=ALU.subtract).then_inc(low_ready, 1)
                        for k in range(2):
                            dve.wait_ge(v_done, 4 * i + 2 * par + k + 1)
                            nc.vector.tensor_tensor(
                                v_sb[:, ds((2 * i + par) * SUB + 2 * k, 2), :],
                                v_ps[k][:, :].rearrange("p (s n) -> p s n", s=2), bias_v[:, :, :],
                                ALU.add).then_inc(v_ready, 1)

                pairwise(dve, pair)

        with ExitStack() as stage:
            sb, bank, sem = allocators(stage)
            CHUNKS = N // BANK
            CONV = 1024
            CONVS = N // CONV
            SCORES, TURNS = 2, 4
            UNITS = TILES * HEADS
            STEPS = 8

            k_stack = [sb(f"k_stack{h}", [P, N], fp32r) for h in range(GROUP)]
            q_stack = [sb(f"q_stack{i}", [P, GROUP, P], fp32r) for i in range(2)]
            exps = [sb(f"exps{i}", [P, N]) for i in range(4)]
            mask = [sb(f"mask{i}", [P, N], bf16) for i in range(2)]
            adj_part = [sb(f"adj_part{i}", [P, CONV], i32) for i in range(2)]
            adj_diag = sb("adj_diag", [P, P], i32)
            ident_i = sb("ident_i", [P, P], i32)
            mask_diag = sb("mask_diag", [P, P], bf16)
            turned_sb = [sb(f"turned_sb{i}", [P, BANK]) for i in range(4)]
            part_max = sb("part_max", [P, 2, CHUNKS])
            row_max = sb("row_max", [P, 2])
            neg_max = sb("neg_max", [P, 4])
            half_sums = sb("half_sums", [P, 4, 2])
            row_sum = sb("row_sum", [P, 4])
            inv_sum = sb("inv_sum", [P, 4])
            fold = sb("fold", [P, DK])
            ctx_cols = sb("ctx_cols", [P, P])
            ctx_rows = [sb(f"ctx_rows{i}", [P, P]) for i in range(2)]

            score_ps = [bank(f"score_ps{i}") for i in range(SCORES)]
            turn_ps = [bank(f"turn_ps{i}") for i in range(TURNS)]
            ctx_ps = [bank(f"ctx_ps{i}") for i in range(2)]

            k_in = [sem(f"k_in{h}") for h in range(GROUP)]
            q_in = [sem(f"q_in{i}") for i in range(2)]
            adj_in = [sem(f"adj_in{i}") for i in range(2)]
            diag_in = sem("diag_in")
            adj_used = sem("adj_used")
            diag_step = sem("diag_step")
            mask_ready = sem("mask_ready")
            scored = sem("scored")
            masked = sem("masked")
            max_found = sem("max_found")
            max_ready = sem("max_ready")
            exped = sem("exped")
            turned = sem("turned")
            act_copied = sem("act_copied")
            dve_copied = sem("dve_copied")
            weighed = sem("weighed")
            ctx_copied = sem("ctx_copied")
            folded = sem("folded")
            sum_found = sem("sum_found")
            inv_ready = sem("inv_ready")
            normed = sem("normed")
            ctx_stored = [sem(f"ctx_stored{i}") for i in range(2)]
            fold_made = sem("fold_made")

            BEHIND = 3
            DVE_GROUPS = (0, 4)
            ACT_GROUPS = tuple(c for c in range(CHUNKS) if c not in DVE_GROUPS)

            def wait_copied(eng, unit, c):
                if c in DVE_GROUPS:
                    eng.wait_ge(dve_copied, len(DVE_GROUPS) * unit + DVE_GROUPS.index(c) + 1)
                else:
                    eng.wait_ge(act_copied, len(ACT_GROUPS) * unit + ACT_GROUPS.index(c) + 1)

            def every_step(eng, step, ahead_of_loop=None):
                for u in range(2):
                    step(u, u, u)
                half = UNITS // GROUPS
                for g in range(GROUPS):
                    first = 2 if g == 0 else g * half + 2
                    for u in range(first, first + STEPS - 2 if g == 0 else first + 6):
                        step(u, u % STEPS, u)
                    start = g * half + STEPS
                    if ahead_of_loop:
                        ahead_of_loop(start)
                    with eng.Fori(0, (half - STEPS) // STEPS) as i:
                        for j in range(STEPS):
                            step(start + STEPS * i + j, j, None)
                    if g < GROUPS - 1:
                        for u in range((g + 1) * half, (g + 1) * half + 2):
                            step(u, u % STEPS, u)
                for u in range(UNITS, UNITS + 5):
                    step(u, u % STEPS, u)

            def has(u, lag):
                return not isinstance(u, int) or 0 <= u - lag < UNITS

            def group_of(n, lag):
                return 0 if n - lag < UNITS // GROUPS else 1

            block = stage.enter_context(nc.Block())

            @block.sync
            def _(sp):
                def load_k(g):
                    for h in range(GROUP):
                        if g:
                            sp.wait_ge(scored, CHUNKS * (g * UNITS // GROUPS - GROUP + h + 1))
                        rows = ds((g * GROUP + h) * DK, DK)
                        for r in range(HALVES):
                            sp.dma_start(k_stack[h][r * DK:(r + 1) * DK, :].bitcast(fp32), k_halves[r, rows, :]).then_inc(k_in[h], 16)

                adj_used_next = expected(sp)

                def load_tile(g, tg, par, first):
                    t = g * TILES + tg
                    if not first:
                        sp.wait_ge(scored, CHUNKS * GROUP * (t - 1))
                    for r in range(HALVES):
                        src = q_halves[r, g * P:(g + 1) * P, ds(tg * P, P)].rearrange("(h d) n -> d h n", d=DK)
                        sp.dma_start(q_stack[par][r * DK:(r + 1) * DK, :, :].bitcast(fp32), src).then_inc(q_in[par], 16)
                    if not (first and par == 0):
                        sp.wait_ge(mask_ready, t)
                    sp.dma_start(adj_diag[:, :], adj[ds(tg * P, P), ds(tg * P, P)]).then_inc(diag_in, 16)
                    for c in range(CONVS):
                        if not isinstance(t, int):
                            wait_then_add(sp, adj_used, adj_used_next, 1)
                        elif t > 0 or c >= 2:
                            sp.wait_ge(adj_used, CONVS * t + c - 1)
                        sp.dma_start(adj_part[c % 2][:, :],
                                     adj[ds(tg * P, P), c * CONV:(c + 1) * CONV]).then_inc(adj_in[c % 2], 16)

                for g in range(GROUPS):
                    if g == 0:
                        load_k(0)
                    for par in range(2):
                        load_tile(g, par, par, g == 0)
                    if g:
                        load_k(g)
                    sp.reg_mov(adj_used_next, CONVS * (g * TILES + 2) - 1)
                    with sp.Fori(1, TILES // 2) as i:
                        for par in range(2):
                            load_tile(g, 2 * i + par, par, False)

            @block.gpsimd
            def _(pool):
                added_next, ready_next, masked_next = expected(pool), expected(pool), expected(pool)
                adj_in_next = [expected(pool) for _ in range(2)]

                def convert_tile(g, tg, par, first):
                    t = g * TILES + tg
                    looped = not isinstance(t, int)
                    pool.wait_ge(diag_in, 16 * t + 16)
                    pool.wait_ge(diag_step, 3 * t + 1)
                    nc.gpsimd.tensor_tensor(adj_diag[:, :], adj_diag[:, :], ident_i[:, :],
                                            ALU.add).then_inc(diag_step, 1)
                    if looped:
                        wait_then_add(pool, mask_ready, ready_next, 1)
                        wait_then_add(pool, diag_step, added_next, 3)
                    else:
                        pool.wait_ge(diag_step, 3 * t + 2)
                        if t > 0:
                            pool.wait_ge(mask_ready, t)
                    nc.gpsimd.tensor_scalar(mask_diag[:, :], adj_diag[:, :], 0.0, MASKED, ALU.is_equal,
                                            ALU.mult).then_inc(diag_step, 1)
                    for c in range(CONVS):
                        if looped:
                            wait_then_add(pool, adj_in[c % 2], adj_in_next[c % 2], 16)
                            wait_then_add(pool, masked, masked_next,
                                          CHUNKS // CONVS if c < CONVS - 1
                                          else CHUNKS * GROUP - (CONVS - 1) * CHUNKS // CONVS)
                        else:
                            pool.wait_ge(adj_in[c % 2], 16 * (CONVS // 2) * t + 16 * (c // 2) + 16)
                            if t >= 2:
                                pool.wait_ge(masked, last_use(t) + (c + 1) * CHUNKS // CONVS)
                        nc.gpsimd.tensor_scalar(mask[par][:, c * CONV:(c + 1) * CONV], adj_part[c % 2][:, :],
                                                0.0, MASKED, ALU.is_equal, ALU.mult).then_inc(adj_used, 1)
                    pool.wait_ge(adj_used, CONVS * t + CONVS)
                    pool.wait_ge(diag_step, 3 * t + 3)
                    nc.gpsimd.tensor_copy(mask[par][:, ds(tg * P, P)], mask_diag[:, :]).then_inc(diag_step, 1)
                    pool.wait_ge(diag_step, 3 * t + 4)
                    pool.sem_inc(mask_ready, 1)

                def last_use(t):
                    return CHUNKS * (GROUP * (t - 1) - 1)

                for g in range(GROUPS):
                    for par in range(2):
                        convert_tile(g, par, par, g == 0)
                    t = g * TILES + 2
                    pool.reg_mov(ready_next, t)
                    pool.reg_mov(added_next, 3 * t + 2)
                    pool.reg_mov(masked_next, last_use(t) + CHUNKS // CONVS)
                    for k in range(2):
                        pool.reg_mov(adj_in_next[k], 16 * (CONVS // 2) * t + 16)
                    with pool.Fori(1, TILES // 2) as i:
                        for par in range(2):
                            convert_tile(g, 2 * i + par, par, False)

            @block.tensor
            def _(pe):
                def step(u, m, n):
                    h = m % GROUP
                    par = m // GROUP
                    for c in range(CHUNKS):
                        if has(u, 0):
                            if c == 0 and h == 0:
                                pe.wait_ge(q_in[par], 8 * (u - m) + 16 * HALVES)
                            if c == 0 and n is not None and n % (UNITS // GROUPS) < GROUP:
                                pe.wait_ge(k_in[h], 16 * HALVES * (group_of(n, 0) + 1))
                            if n is None or n > 0 or c >= SCORES:
                                pe.wait_ge(masked, CHUNKS * u + c - SCORES + 1)
                            nc.tensor.matmul(score_ps[c % SCORES][:, :], q_stack[par][:, h, :],
                                             k_stack[h][:, c * BANK:(c + 1) * BANK],
                                             start=True, stop=True).then_inc(scored, 1)
                        if has(u, 2):
                            v = u - 2
                            if c % (CHUNKS // 2) == 0:
                                pe.wait_ge(exped, 2 * v + c // (CHUNKS // 2) + 1)
                            if c >= TURNS:
                                wait_copied(pe, v, c - TURNS)
                            elif n is None or n > 2:
                                wait_copied(pe, v - 1, c + CHUNKS - TURNS)
                            for j in range(SUB):
                                kt = c * SUB + j
                                last = nc.tensor.transpose(turn_ps[c % TURNS][:, j * P:(j + 1) * P],
                                                           exps[(m - 2) % 4][:, kt * P:(kt + 1) * P], ident[:, :])
                            last.then_inc(turned, 1)
                        lag, gr = (2, c - BEHIND) if c >= BEHIND else (3, c + CHUNKS - BEHIND)
                        if has(u, lag):
                            v = u - lag
                            wait_copied(pe, v, gr)
                            if gr == 0:
                                if n is None or n > 3:
                                    pe.wait_ge(normed, v - 1)
                            head, side = (m - lag) % GROUP, (m - lag) % 2
                            for j in range(SUB):
                                kt = gr * SUB + j
                                last = nc.tensor.matmul(
                                    ctx_ps[side][j * DK:(j + 1) * DK, 0:P],
                                    v_heads(n, lag, kt, head),
                                    turned_sb[gr % 4][:, j * P:(j + 1) * P],
                                    start=(gr == 0), stop=(gr == CHUNKS - 1), tile_position=(0, j * DK))
                            last.then_inc(weighed, 1)
                        if c == BEHIND + 2 and has(u, 3):
                            v = u - 3
                            pe.wait_ge(ctx_copied, v + 1)
                            nc.tensor.matmul(ctx_ps[(m - 3) % 2][:, P:P + DK], ctx_cols[:, :], fold[:, :],
                                             start=True, stop=True).then_inc(folded, 1)

                loop_group = [0]

                def v_heads(n, lag, kt, head):
                    g = group_of(n, lag) if n is not None else loop_group[0]
                    f = (g * GROUP + head) * DK
                    return v_sb[:, kt, f:f + DK]

                def counted(u, m, n):
                    if n is not None:
                        loop_group[0] = group_of(n, 0)
                    step(u, m, n)

                pe.wait_ge(fold_made, GROUP)
                every_step(pe, counted)

            @block.scalar
            def _(act):
                def step(u, m, n):
                    for half in range(2):
                        if has(u, 1):
                            v, b = u - 1, (m - 1) % 4
                            if half == 0:
                                act.wait_ge(max_ready, v + 1)
                            cols = slice(half * N // 2, (half + 1) * N // 2)
                            nc.scalar.activation(exps[b][:, cols], exps[b][:, cols], ACT.Exp,
                                                 bias=neg_max[:, b:b + 1], scale=SCALE,
                                                 accum_out=half_sums[:, b, half:half + 1]).then_inc(exped, 1)
                        if has(u, 2):
                            v = u - 2
                            for c in ACT_GROUPS:
                                if c // (CHUNKS // 2) != half:
                                    continue
                                act.wait_ge(turned, CHUNKS * v + c + 1)
                                if n is None or n > 2 or c >= 4:
                                    act.wait_ge(weighed, CHUNKS * v + c - 3)
                                nc.scalar.activation(turned_sb[c % 4][:, :], turn_ps[c % TURNS][:, :],
                                                     ACT.Copy).then_inc(act_copied, 1)
                        if half == 0 and m % GROUP == 0 and (n is None or n >= 8):
                            act.wait_ge(normed, u - 4)
                            store(u - 8, n, (m % STEPS) // GROUP)

                def store(v, n, par):
                    g = group_of(n, 8) if n is not None else loop_group[0]
                    row = (v - g * (UNITS // GROUPS)) * (P // GROUP)
                    act.dma_start(ctx_dram[ds(row, P), g * P:(g + 1) * P],
                                  ctx_rows[par][:, :]).then_inc(ctx_stored[par], 16)

                loop_group = [0]

                def counted(u, m, n):
                    if n is not None:
                        loop_group[0] = group_of(n, 0)
                    step(u, m, n)

                every_step(act, counted)
                for par in range(2):
                    act.wait_ge(ctx_stored[par], 16 * TILES * GROUPS // 2)

            @block.vector
            def _(dve):
                nc.vector.tensor_copy(ident_i[:, :], ident[:, :]).then_inc(diag_step, 1)
                for j in range(GROUP):
                    nc.vector.tensor_copy(fold[j * DK:(j + 1) * DK, :],
                                          ident[j * DK:(j + 1) * DK, j * DK:(j + 1) * DK]).then_inc(fold_made, 1)
                scored_next = expected(dve)

                def step(u, m, n):
                    h, par = m % GROUP, m // GROUP
                    for c in range(CHUNKS):
                        if has(u, 0):
                            if c == 0:
                                if h == 0:
                                    dve.wait_ge(mask_ready, tile_count(u - m, par))
                                if n is None or n >= 4:
                                    dve.wait_ge(turned, CHUNKS * (u - 3))
                            if n is None:
                                wait_then_add(dve, scored, scored_next, 1)
                            else:
                                dve.wait_ge(scored, CHUNKS * u + c + 1)
                            cols = slice(c * BANK, (c + 1) * BANK)
                            nc.vector.tensor_tensor_reduce(
                                out=exps[m % 4][:, cols], in0=score_ps[c % SCORES][:, :], in1=mask[par][:, cols],
                                scale=1.0, scalar=LOWEST, op0=ALU.add, op1=ALU.max,
                                accum_out=part_max[:, m % 2, c:c + 1]).then_inc(masked, 1)
                        if c in DVE_GROUPS and has(u, 2):
                            v = u - 2
                            dve.wait_ge(turned, CHUNKS * v + c + 1)
                            if n is None or n > 2 or c >= 4:
                                dve.wait_ge(weighed, CHUNKS * v + c - 3)
                            nc.vector.tensor_copy(turned_sb[c % 4][:, :], turn_ps[c % TURNS][:, :]).then_inc(dve_copied, 1)
                        if c == 1 and has(u, 2):
                            v, b = u - 2, (m - 2) % 4
                            dve.wait_ge(exped, 2 * v + 2)
                            nc.vector.tensor_tensor(row_sum[:, b:b + 1], half_sums[:, b, 0:1],
                                                    half_sums[:, b, 1:2], ALU.add).then_inc(sum_found, 1)
                        if c == 3 and has(u, 2):
                            v, b = u - 2, (m - 2) % 4
                            dve.wait_ge(sum_found, v + 1)
                            nc.vector.reciprocal(inv_sum[:, b:b + 1], row_sum[:, b:b + 1]).then_inc(inv_ready, 1)
                        if c == BEHIND and has(u, 3):
                            v, side = u - 3, (m - 3) % 2
                            dve.wait_ge(weighed, CHUNKS * (v + 1))
                            if n is None or n > 3:
                                dve.wait_ge(folded, v)
                            nc.vector.tensor_copy(ctx_cols[:, :], ctx_ps[side][:, 0:P]).then_inc(ctx_copied, 1)
                        if c == BEHIND + 4 and has(u, 3):
                            v, b = u - 3, (m - 3) % 4
                            tile_par = ((m - 3) % STEPS) // GROUP
                            dve.wait_ge(folded, v + 1)
                            dve.wait_ge(inv_ready, v + 1)
                            if b == 0 and (n is None or n > 8):
                                dve.wait_ge(ctx_stored[tile_par], 2 * (v - (m - 3) % STEPS))
                            nc.vector.tensor_scalar(ctx_rows[tile_par][:, b * DK:(b + 1) * DK], ctx_ps[(m - 3) % 2][:, P:P + DK],
                                                    inv_sum[:, b:b + 1], None, ALU.mult).then_inc(normed, 1)
                    if has(u, 0):
                        dve.wait_ge(masked, CHUNKS * u + CHUNKS)
                        nc.vector.reduce_max(row_max[:, m % 2:m % 2 + 1], part_max[:, m % 2, :],
                                             AX.X).then_inc(max_found, 1)
                        dve.wait_ge(max_found, u + 1)
                        nc.vector.tensor_scalar(neg_max[:, m % 4:m % 4 + 1], row_max[:, m % 2:m % 2 + 1], -SCALE,
                                                None, ALU.mult).then_inc(max_ready, 1)

                def tile_count(first, par):
                    if isinstance(first, int):
                        return first // GROUP + par + 1
                    return tiles_before[0] + par + 1

                tiles_before = [0]

                def counted(u, m, n):
                    if n is None:
                        tiles_before[0] = (u - m) // GROUP
                    step(u, m, n)

                every_step(dve, counted, lambda start: dve.reg_mov(scored_next, CHUNKS * start + 1))

        with ExitStack() as stage:
            sb, bank, sem = allocators(stage)
            wo_rows = sb("wo_rows", [P, KB, D])
            w1_rows = sb("w1_rows", [P, FB, D])
            w2_rows = sb("w2_rows", [P, KB, FF])
            wo_cols = sb("wo_cols", [P, KB, D])
            w1_cols = sb("w1_cols", [P, KB, FF])
            w2_cols = sb("w2_cols", [P, FB, D])
            row_names = {"bo": bo, "b2": b2, "g1": ln1_g, "s1": ln1_b, "g2": ln2_g, "s2": ln2_b}
            rows_of = {k: sb(f"row_{k}", [P, D]) for k in row_names}
            b1_cols = sb("b1_cols", [P, FB])
            ctx_in_sb = [sb(f"ctx_in_sb{i}", [P, SUB, D]) for i in range(2)]
            x_in_sb = [sb(f"x_in_sb{i}", [P, SUB, D]) for i in range(2)]
            ctx_t = sb("ctx_t", [P, KB, BANK])
            h1 = [sb(f"h1_{i}", [P, SUB, D]) for i in range(2)]
            h1_t = [sb(f"h1_t{i}", [P, KB, BANK]) for i in range(2)]
            hidden = sb("hidden", [P, FB, BANK])
            pre = [sb(f"pre{i}", [P, SUB, D]) for i in range(2)]
            stats = [sb(f"stats{i}", [P, SUB, 6]) for i in range(2)]
            mean_var = [sb(f"mean_var{i}", [P, SUB, 2]) for i in range(2)]
            var_eps = [sb(f"var_eps{i}", [P, SUB]) for i in range(2)]
            idle = sb("idle", [P, 1])
            std = [sb(f"std{i}", [P, SUB]) for i in range(2)]
            std_inv = [sb(f"std_inv{i}", [P, SUB]) for i in range(2)]
            newton = [sb(f"newton{i}", [P, SUB]) for i in range(2)]
            final = [sb(f"final{i}", [P, SUB, D]) for i in range(2)]
            turn_ps = [bank(f"c_turn_ps{i}") for i in range(2)]
            wo_ps = [bank(f"wo_ps{i}") for i in range(2)]
            up_ps = [bank(f"up_ps{i}") for i in range(2)]
            down_ps = [bank(f"down_ps{i}") for i in range(2)]

            wts_in = sem("wts_in")
            rows_in = sem("rows_in")
            wt_turned = sem("wt_turned")
            wt_copied = sem("wt_copied")
            ctx_in = [sem(f"ctx_in{i}") for i in range(2)]
            xr_in = [sem(f"xr_in{i}") for i in range(2)]
            c_turned = sem("c_turned")
            c_copied = sem("c_copied")
            wo_done = sem("wo_done")
            wo_read = sem("wo_read")
            h1_ready = sem("h1_ready")
            up_done = sem("up_done")
            up_read = sem("up_read")
            down_done = sem("down_done")
            down_read = sem("down_read")
            ln_step = sem("ln_step")
            std_ready = sem("std_ready")
            final_ready = sem("final_ready")
            out_stored = [sem(f"out_stored{i}") for i in range(2)]
            PAIRS = BLOCKS // 2

            block = stage.enter_context(nc.Block())

            @block.sync
            def _(sp):
                sp.dma_start(wo_rows[:, :, :], Wo.rearrange("(f p) d -> p f d", p=P)).then_inc(wts_in, 16)
                sp.dma_start(w1_rows[:, :, :], W1.rearrange("(f p) d -> p f d", p=P)).then_inc(wts_in, 16)
                sp.dma_start(w2_rows[:, :, :], W2.rearrange("(f p) d -> p f d", p=P)).then_inc(wts_in, 16)
                for k, a in row_names.items():
                    sp.dma_start(rows_of[k][:, :], a.partition_broadcast(P)).then_inc(rows_in, 16)
                with nc.allow_non_contiguous_dma(reason="eight columns of biases"):
                    sp.dma_start(b1_cols[:, :], b1.rearrange("(f p) -> p f", p=P)).then_inc(rows_in, 16)

                def load(b, par, first):
                    if not first:
                        sp.wait_ge(wo_read, 2 * b - 2)
                    sp.dma_start(ctx_in_sb[par][:, :, :], token_block(ctx_dram, b)).then_inc(ctx_in[par], 16)
                    sp.dma_start(x_in_sb[par][:, :, :], token_block(x, b)).then_inc(xr_in[par], 16)

                def store(b, par):
                    sp.wait_ge(final_ready, b + 1)
                    sp.dma_start(token_block(out, b), final[par][:, :, :]).then_inc(out_stored[par], 16)

                for par in range(2):
                    load(par, par, True)
                with sp.Fori(0, PAIRS - 1) as i:
                    for par in range(2):
                        load(2 * i + 2 + par, par, False)
                        store(2 * i + par, par)
                for par in range(2):
                    store(BLOCKS - 2 + par, par)
                for par in range(2):
                    sp.wait_ge(out_stored[par], 16 * PAIRS)

            NORM = 2 + 16

            def ln1_before(b):
                return NORM * (2 * b - 1)

            def ln2_before(b, last_block):
                return NORM * (2 * b + (1 if last_block else 2))

            def blockwise(eng, step):
                for b in range(3):
                    step(b, b % 2, b == 0, False)
                with eng.Fori(0, (BLOCKS - 4) // 2) as i:
                    for j in range(2):
                        step(2 * i + 3 + j, (3 + j) % 2, False, False)
                step(BLOCKS - 1, 1, False, True)

            @block.tensor
            def _(pe):
                pe.wait_ge(wts_in, 48)
                n = 0
                for rows, cols, nf in ((wo_rows, wo_cols, KB), (w1_rows, w1_cols, FB)):
                    for f0 in range(0, nf, 2):
                        if n >= 2:
                            pe.wait_ge(wt_copied, n - 1)
                        for c in range(KB):
                            for f in range(2):
                                last = nc.tensor.transpose(turn_ps[n % 2][:, (2 * c + f) * P:(2 * c + f + 1) * P],
                                                           rows[:, f0 + f, c * P:(c + 1) * P], ident[:, :])
                        last.then_inc(wt_turned, 1)
                        n += 1
                for m0 in range(0, FB, 2):
                    pe.wait_ge(wt_copied, n - 1)
                    for m in range(2):
                        for f in range(KB):
                            last = nc.tensor.transpose(turn_ps[n % 2][:, (2 * m + f) * P:(2 * m + f + 1) * P],
                                                       w2_rows[:, f, (m0 + m) * P:(m0 + m + 1) * P], ident[:, :])
                    last.then_inc(wt_turned, 1)
                    n += 1
                pe.wait_ge(wt_copied, n)

                def project(b, par, first):
                    pe.wait_ge(ctx_in[par], 8 * (b - par) + 16)
                    for c in range(KB):
                        if not first:
                            pe.wait_ge(c_copied, 4 * b)
                        for s in range(SUB):
                            last = nc.tensor.transpose(turn_ps[c][:, s * P:(s + 1) * P],
                                                       ctx_in_sb[par][:, s, c * P:(c + 1) * P], ident[:, :])
                        last.then_inc(c_turned, 1)
                    pe.wait_ge(c_copied, 4 * b + 2)
                    for k in range(2):
                        if not first:
                            pe.wait_ge(wo_read, 2 * b)
                        for s in range(2):
                            for c in range(KB):
                                last = nc.tensor.matmul(wo_ps[k][:, s * D:(s + 1) * D],
                                                        ctx_t[:, c, (2 * k + s) * P:(2 * k + s + 1) * P],
                                                        wo_cols[:, c, :], start=(c == 0), stop=(c == KB - 1))
                        last.then_inc(wo_done, 1)

                def turn_h1(b, par):
                    pe.wait_ge(h1_ready, b + 1)
                    for c in range(KB):
                        for s in range(SUB):
                            last = nc.tensor.transpose(turn_ps[c][:, s * P:(s + 1) * P],
                                                       h1[par][:, s, c * P:(c + 1) * P], ident[:, :])
                        last.then_inc(c_turned, 1)

                def up(b, par, first):
                    pe.wait_ge(c_copied, 4 * b + 4)
                    for m in range(FB):
                        if not (first and m < 2):
                            pe.wait_ge(up_read, FB * b + m - 1)
                        for c in range(KB):
                            last = nc.tensor.matmul(up_ps[m % 2][:, :], w1_cols[:, c, m * P:(m + 1) * P],
                                                    h1_t[par][:, c, :], start=(c == 0), stop=(c == KB - 1))
                        last.then_inc(up_done, 1)

                def down(b, first):
                    pe.wait_ge(up_read, FB * b + FB)
                    for k in range(2):
                        if not first:
                            pe.wait_ge(down_read, 2 * b)
                        for s in range(2):
                            for m in range(FB):
                                last = nc.tensor.matmul(down_ps[k][:, s * D:(s + 1) * D],
                                                        hidden[:, m, (2 * k + s) * P:(2 * k + s + 1) * P],
                                                        w2_cols[:, m, :], start=(m == 0), stop=(m == FB - 1))
                        last.then_inc(down_done, 1)

                project(0, 0, True)
                turn_h1(0, 0)

                def step(b, par, first, last):
                    if not last:
                        project(b + 1, 1 - par, False)
                    up(b, par, first)
                    down(b, first)
                    if not last:
                        turn_h1(b + 1, 1 - par)

                blockwise(pe, step)

            @block.scalar
            def _(act):
                n = 0
                for cols, nf in ((wo_cols, KB), (w1_cols, FB)):
                    for f0 in range(0, nf, 2):
                        act.wait_ge(wt_turned, n + 1)
                        nc.scalar.activation(cols[:, :, f0 * P:(f0 + 2) * P],
                                             turn_ps[n % 2][:, :].rearrange("p (c n) -> p c n", c=KB),
                                             ACT.Copy).then_inc(wt_copied, 1)
                        n += 1
                for m0 in range(0, FB, 2):
                    act.wait_ge(wt_turned, n + 1)
                    nc.scalar.activation(w2_cols[:, m0:m0 + 2, :],
                                         turn_ps[n % 2][:, :].rearrange("p (m n) -> p m n", m=2),
                                         ACT.Copy).then_inc(wt_copied, 1)
                    n += 1
                act.wait_ge(rows_in, 16 * (len(row_names) + 1))

                def ctx_copy(b, first):
                    for c in range(KB):
                        act.wait_ge(c_turned, 4 * b + c + 1)
                        if not first:
                            act.wait_ge(wo_done, 2 * b)
                        nc.scalar.activation(ctx_t[:, c, :], turn_ps[c][:, :], ACT.Copy).then_inc(c_copied, 1)

                def h1_copy(b, par, early):
                    for c in range(KB):
                        act.wait_ge(c_turned, 4 * b + c + 3)
                        if not early:
                            act.wait_ge(up_done, FB * (b - 1))
                        nc.scalar.activation(h1_t[par][:, c, :], turn_ps[c][:, :], ACT.Copy).then_inc(c_copied, 1)

                def root(w, before):
                    act.wait_ge(ln_step, before + 11)
                    nc.scalar.activation(std[w][:, :], var_eps[w][:, :], ACT.Sqrt).then_inc(std_ready, 1)

                ctx_copy(0, True)
                root(0, 0)
                h1_copy(0, 0, True)

                def step(b, par, first, last):
                    if not last:
                        ctx_copy(b + 1, False)
                    for m in range(FB):
                        if m == 2 and not first:
                            root(1, ln2_before(b - 1, False))
                        act.wait_ge(up_done, FB * b + m + 1)
                        if not first:
                            act.wait_ge(down_done, 2 * b)
                        nc.scalar.activation(hidden[:, m, :], up_ps[m % 2][:, :], ACT.Relu,
                                             bias=b1_cols[:, m:m + 1]).then_inc(up_read, 1)
                    if not last:
                        root(0, ln1_before(b + 1))
                        h1_copy(b + 1, 1 - par, first)

                blockwise(act, step)
                root(1, ln2_before(BLOCKS - 1, True))

            @block.vector
            def _(dve):
                def norm(w, done, which, gain, shift, to, end):
                    for s in range(SUB):
                        nc.vector.bn_stats(stats[w][:, s, :], pre[w][:, s, :]).then_inc(ln_step, 1)
                    dve.wait_ge(ln_step, done + 4)
                    nc.vector.memset(idle[:, :], 0.0)
                    for s in range(SUB):
                        nc.vector.bn_aggr(mean_var[w][:, s, :], stats[w][:, s, :]).then_inc(ln_step, 1)
                    dve.wait_ge(ln_step, done + 8)
                    nc.vector.tensor_scalar(var_eps[w][:, :], mean_var[w][:, :, 1], EPS, None,
                                            ALU.add).then_inc(ln_step, 1)
                    dve.wait_ge(std_ready, which + 1)
                    nc.vector.reciprocal(std_inv[w][:, :], std[w][:, :]).then_inc(ln_step, 1)
                    dve.wait_ge(ln_step, done + 10)
                    nc.vector.tensor_tensor(newton[w][:, :], std_inv[w][:, :], std_inv[w][:, :],
                                            ALU.mult).then_inc(ln_step, 1)
                    dve.wait_ge(ln_step, done + 11)
                    nc.vector.tensor_tensor(newton[w][:, :], newton[w][:, :], var_eps[w][:, :],
                                            ALU.mult).then_inc(ln_step, 1)
                    dve.wait_ge(ln_step, done + 12)
                    nc.vector.tensor_scalar(newton[w][:, :], newton[w][:, :], -0.5, 1.5, ALU.mult,
                                            ALU.add).then_inc(ln_step, 1)
                    dve.wait_ge(ln_step, done + 13)
                    nc.vector.tensor_tensor(std_inv[w][:, :], std_inv[w][:, :], newton[w][:, :],
                                            ALU.mult).then_inc(ln_step, 1)
                    dve.wait_ge(ln_step, done + 14)
                    for s in range(SUB):
                        last = nc.vector.tensor_scalar(to[:, s, :], pre[w][:, s, :], mean_var[w][:, s, 0:1],
                                                       std_inv[w][:, s:s + 1], ALU.subtract, ALU.mult)
                    last.then_inc(ln_step, 1)
                    dve.wait_ge(ln_step, done + 15)
                    for s in range(SUB):
                        last = nc.vector.tensor_tensor(to[:, s, :], to[:, s, :], rows_of[gain][:, :], ALU.mult)
                    last.then_inc(ln_step, 1)
                    dve.wait_ge(ln_step, done + 16)
                    for s in range(SUB):
                        last = nc.vector.tensor_tensor(to[:, s, :], to[:, s, :], rows_of[shift][:, :], ALU.add)
                    last.then_inc(end, 1)

                def ln1(b, par, early):
                    done = 0 if early else ln1_before(b)
                    dve.wait_ge(xr_in[par], 8 * (b - par) + 16)
                    for k in range(2):
                        dve.wait_ge(wo_done, 2 * b + k + 1)
                        for s in range(2):
                            last = nc.vector.tensor_tensor(pre[0][:, 2 * k + s, :], wo_ps[k][:, s * D:(s + 1) * D],
                                                           rows_of["bo"][:, :], ALU.add)
                        last.then_inc(ln_step, 1)
                    dve.wait_ge(ln_step, done + 2)
                    for k in range(2):
                        last = nc.vector.tensor_tensor(pre[0][:, 2 * k:2 * k + 2, :], pre[0][:, 2 * k:2 * k + 2, :],
                                                       x_in_sb[par][:, 2 * k:2 * k + 2, :], ALU.add)
                        last.then_inc(wo_read, 1)
                    dve.wait_ge(wo_read, 2 * b + 2)
                    norm(0, done + 2, 0 if early else 2 * b - 1, "g1", "s1", h1[par], h1_ready)

                def ln2(b, par, early, last_block):
                    done = ln2_before(b, last_block)
                    dve.wait_ge(h1_ready, b + 1)
                    for k in range(2):
                        dve.wait_ge(down_done, 2 * b + k + 1)
                        for s in range(2):
                            last = nc.vector.tensor_tensor(pre[1][:, 2 * k + s, :], down_ps[k][:, s * D:(s + 1) * D],
                                                           rows_of["b2"][:, :], ALU.add)
                        last.then_inc(ln_step, 1)
                    dve.wait_ge(ln_step, done + 2)
                    for k in range(2):
                        last = nc.vector.tensor_tensor(pre[1][:, 2 * k:2 * k + 2, :], pre[1][:, 2 * k:2 * k + 2, :],
                                                       h1[par][:, 2 * k:2 * k + 2, :], ALU.add)
                        last.then_inc(down_read, 1)
                    dve.wait_ge(down_read, 2 * b + 2)
                    if not early:
                        dve.wait_ge(out_stored[par], 8 * (b - par))
                    norm(1, done + 2, 2 * b + (1 if last_block else 2), "g2", "s2", final[par], final_ready)

                dve.wait_ge(rows_in, 16 * (len(row_names) + 1))
                ln1(0, 0, True)

                def step(b, par, first, last):
                    if not first:
                        ln2(b - 1, 1 - par, isinstance(b, int) and b < 3, False)
                    if not last:
                        ln1(b + 1, 1 - par, False)

                blockwise(dve, step)
                ln2(BLOCKS - 1, 1, False, True)


_INS = ["x", "adj", "L0_gnn_Wq", "L0_gnn_bq", "L0_gnn_Wk", "L0_gnn_bk", "L0_gnn_Wv", "L0_gnn_bv", "L0_gnn_Wo",
        "L0_gnn_bo", "L0_gnn_W1", "L0_gnn_b1", "L0_gnn_W2", "L0_gnn_b2", "L0_gnn_ln1_g", "L0_gnn_ln1_b",
        "L0_gnn_ln2_g", "L0_gnn_ln2_b"]


def kernel(**inputs):
    import numpy as _np
    import concourse.bacc as _bacc
    from concourse import mybir as _mybir
    from concourse.bass_utils import run_bass_kernel_spmd as _run

    nc = _bacc.Bacc("TRN2", target_bir_lowering=False, num_devices=1)
    arrays, args = {}, []
    for name in _INS:
        a = _np.ascontiguousarray(inputs[name])
        arrays[f"in_{name}"] = a
        args.append(nc.dram_tensor(f"in_{name}", a.shape, _mybir.dt.from_np(a.dtype), kind="ExternalInput").ap())
    out = nc.dram_tensor("out_h2", inputs["x"].shape, _mybir.dt.float32, kind="ExternalOutput").ap()
    build_gnn_layer(nc, *args, out)
    r = _run(nc, [arrays], core_ids=[0])
    return r.results[0]["out_h2"]
```

```python
import concourse.bass as bass
from concourse import mybir
from contextlib import ExitStack


def build_gnn_layer(nc, x, adj, Wq, bq, Wk, bk, Wv, bv, Wo, bo, W1, b1, W2, b2,
                    ln1_g, ln1_b, ln2_g, ln2_b, out):
    fp32, fp32r, bf16, i32 = (mybir.dt.float32, mybir.dt.float32r, mybir.dt.bfloat16, mybir.dt.int32)
    ALU, ACT, AX = mybir.AluOpType, mybir.ActivationFunctionType, mybir.AxisListType
    ds = bass.ds

    N, D = x.shape
    FF = W1.shape[0]
    P = 128
    BANK = 512
    HEADS, DK = 8, 32
    GROUP = P // DK
    GROUPS = HEADS // GROUP
    STACK = 4
    K_HALF = (0, 1, 0, 1)
    Q_HALF = (0, 0, 1, 1)
    KB = D // P
    FB = FF // P
    TILES = N // P
    SUB = BANK // P
    BLOCKS = N // BANK
    SCALE = float(DK) ** -0.5
    MASKED = -1.0e9 / SCALE
    LOWEST = -3.0e38
    CHUNKS = N // BANK
    CONV = 1024
    CONVS = N // CONV
    EPS = 1e-5

    k_halves = nc.dram_tensor("k_halves", (2, D, N), fp32, kind="Internal").ap()
    q_halves = nc.dram_tensor("q_halves", (2, D, N), fp32, kind="Internal").ap()
    ctx_dram = nc.dram_tensor("ctx_rows", (N, D), fp32, kind="Internal").ap()

    def expected(eng):
        register = eng.alloc_register()
        eng.reg_mov(register, 0)
        return register

    def wait_then_add(eng, semaphore, register, step):
        eng.wait_ge(semaphore, register)
        eng.reg_alu(register, register, step, ALU.add)

    def allocators(stack):
        def sb(name, shape, dt=fp32):
            return stack.enter_context(nc.sbuf_tensor(name, shape, dt))

        def bank(name):
            return stack.enter_context(nc.psum_tensor(name, [P, BANK], fp32))

        def sem(name):
            return stack.enter_context(nc.semaphore(name))
        return sb, bank, sem

    def token_block(a, b):
        return a[ds(b * BANK, BANK), :].rearrange("(s p) d -> p s d", p=P)

    whole = ExitStack()
    with whole:
        sb, bank, sem = allocators(whole)
        ident = sb("ident", [P, P])
        v_sb = sb("v_sb", [P, TILES, D])

        row_names = {"bo": bo, "b2": b2, "g1": ln1_g, "s1": ln1_b, "g2": ln2_g, "s2": ln2_b}
        with ExitStack() as shared:
            sb, _, _ = allocators(shared)
            w1_rows = sb("w1_rows", [P, FB, D])
            w2_rows = sb("w2_rows", [P, KB, FF])
            wo_rows = sb("wo_rows", [P, KB, D])
            rows_of = {k: sb(f"row_{k}", [P, D]) for k in row_names}
            ctx_in_sb = [sb(f"ctx_in_sb{i}", [P, SUB, D]) for i in range(2)]
            x_in_sb = [sb(f"x_in_sb{i}", [P, SUB, D]) for i in range(2)]
            b1_cols = sb("b1_cols", [P, FB])
        sb, bank, sem = allocators(whole)
        k_stack = [sb(f"k_stack{h}", [P, N], fp32r) for h in range(GROUP)]
        q_stack = [sb(f"q_stack{i}", [P, GROUP, P], fp32r) for i in range(2)]
        mask = [sb(f"mask{i}", [P, N], bf16) for i in range(2)]
        adj_part = [sb(f"adj_part{i}", [P, CONV], i32) for i in range(2)]
        adj_diag = sb("adj_diag", [P, P], i32)
        ident_i = sb("ident_i", [P, P], i32)
        mask_diag = sb("mask_diag", [P, P], bf16)
        q_in = [sem(f"q_in{i}") for i in range(2)]
        adj_in = [sem(f"adj_in{i}") for i in range(2)]
        diag_in = sem("diag_in")
        early_adj_in = [sem(f"early_adj_in{i}") for i in range(2)]
        early_diag_in = sem("early_diag_in")
        adj_used = sem("adj_used")
        diag_step = sem("diag_step")
        mask_ready = sem("mask_ready")
        masked = sem("masked")
        wts_in = sem("wts_in")
        rows_in = sem("rows_in")
        ctx_in = [sem(f"ctx_in{i}") for i in range(2)]
        xr_in = [sem(f"xr_in{i}") for i in range(2)]

        def load_q(sp, g, tg, par):
            for r in range(STACK):
                src = q_halves[Q_HALF[r], g * P:(g + 1) * P, ds(tg * P, P)].rearrange("(h d) n -> d h n", d=DK)
                sp.dma_start(q_stack[par][r * DK:(r + 1) * DK, :, :].bitcast(fp32), src).then_inc(q_in[par], 16)

        def mask_counts(pool):
            return expected(pool), expected(pool), expected(pool), [expected(pool) for _ in range(2)]

        def set_mask_counts(pool, counts, t):
            added_next, ready_next, masked_next, adj_in_next = counts
            pool.reg_mov(ready_next, t)
            pool.reg_mov(added_next, 3 * t + 2)
            pool.reg_mov(masked_next, last_use(t) + CHUNKS // CONVS)
            for k in range(2):
                pool.reg_mov(adj_in_next[k], 16 * (CONVS // 2) * (t - 2) + 16)

        def convert_tile(pool, counts, g, tg, par, after_part=None):
            added_next, ready_next, masked_next, adj_in_next = counts
            t = g * TILES + tg
            diag, part, before = (early_diag_in, early_adj_in, 0) if after_part else (diag_in, adj_in, 2)
            looped = not isinstance(t, int)
            pool.wait_ge(diag, 16 * (t - before) + 16)
            pool.wait_ge(diag_step, 3 * t + 1)
            nc.gpsimd.tensor_tensor(adj_diag[:, :], adj_diag[:, :], ident_i[:, :],
                                    ALU.add).then_inc(diag_step, 1)
            if looped:
                wait_then_add(pool, mask_ready, ready_next, 1)
                wait_then_add(pool, diag_step, added_next, 3)
            else:
                pool.wait_ge(diag_step, 3 * t + 2)
                if t > 0:
                    pool.wait_ge(mask_ready, t)
            nc.gpsimd.tensor_scalar(mask_diag[:, :], adj_diag[:, :], 0.0, MASKED, ALU.is_equal,
                                    ALU.mult).then_inc(diag_step, 1)
            for c in range(CONVS):
                if looped:
                    wait_then_add(pool, adj_in[c % 2], adj_in_next[c % 2], 16)
                    wait_then_add(pool, masked, masked_next,
                                  CHUNKS // CONVS if c < CONVS - 1
                                  else CHUNKS * GROUP - (CONVS - 1) * CHUNKS // CONVS)
                else:
                    pool.wait_ge(part[c % 2], 16 * (CONVS // 2) * (t - before) + 16 * (c // 2) + 16)
                    if t >= 2:
                        pool.wait_ge(masked, last_use(t) + (c + 1) * CHUNKS // CONVS)
                nc.gpsimd.tensor_scalar(mask[par][:, c * CONV:(c + 1) * CONV], adj_part[c % 2][:, :],
                                        0.0, MASKED, ALU.is_equal, ALU.mult).then_inc(adj_used, 1)
                if after_part:
                    after_part(c)
            pool.wait_ge(adj_used, CONVS * t + CONVS)
            pool.wait_ge(diag_step, 3 * t + 3)
            nc.gpsimd.tensor_copy(mask[par][:, ds(tg * P, P)], mask_diag[:, :]).then_inc(diag_step, 1)
            pool.wait_ge(diag_step, 3 * t + 4)
            pool.sem_inc(mask_ready, 1)

        def last_use(t):
            return CHUNKS * (GROUP * (t - 1) - 1)

        with ExitStack() as stage:
            sb, bank, sem = allocators(stage)
            w_rows = [sb(f"w_rows{w}", [P, KB, D]) for w in range(3)]
            w_cols = [sb(f"w_cols{w}", [P, KB, D]) for w in range(3)]
            bias_k = sb("bias_k", [P, KB])
            bias_q = sb("bias_q", [P, KB])
            bias_v = sb("bias_v", [P, 2, D])
            x_rows = [sb(f"x_rows{i}", [P, SUB, D]) for i in range(2)]
            x_cols = [sb(f"x_cols{i}", [P, KB, BANK]) for i in range(2)]
            halves = [[sb(f"halves{i}_{o}", [P, 2, BANK], fp32r) for o in range(1, 4)] for i in range(2)]
            direct = sb("direct", [P, 2, 2 * BANK], fp32r)
            w_ps = [bank(f"w_ps{i}") for i in range(2)]
            x_ps = [bank(f"x_ps{i}") for i in range(2)]
            qk_ps = [bank(f"qk_ps{i}") for i in range(2)]
            v_ps = [bank(f"v_ps{i}") for i in range(2)]

            w_in = sem("w_in")
            bias_in = sem("bias_in")
            ident_zeroed = sem("ident_zeroed")
            ident_ready = sem("ident_ready")
            w_turned = sem("w_turned")
            w_copied = sem("w_copied")
            x_in = [sem(f"x_in{i}") for i in range(2)]
            x_turned = sem("x_turned")
            x_copied = sem("x_copied")
            qk_done = sem("qk_done")
            high_ready = sem("high_ready")
            low_ready = sem("low_ready")
            halves_stored = [sem(f"halves_stored{i}") for i in range(2)]
            direct_stored = sem("direct_stored")
            v_done = sem("v_done")
            v_ready = sem("v_ready")
            PAIRS = BLOCKS // 2
            STORES = 3
            DIRECT = STACK * GROUP

            def half(par, o, which):
                if o == 0:
                    return direct[:, which, par * BANK:(par + 1) * BANK]
                return halves[par][o - 1][:, which, :]

            def pairwise(eng, pair):
                pair(0)
                with eng.Fori(1, PAIRS) as i:
                    pair(i)

            def wait_reused(eng, semaphore, value):
                if not isinstance(value, int) or value > 0:
                    eng.wait_ge(semaphore, value)

            def wait_stored(eng, i, par, o):
                if o == 0 and par == 0:
                    wait_reused(eng, direct_stored, 16 * DIRECT * i)
                elif o == 1:
                    wait_reused(eng, halves_stored[par], 16 * STORES * i)

            block = stage.enter_context(nc.Block())

            @block.gpsimd
            def _(pool):
                nc.gpsimd.memset(ident[:, :], 0.0).then_inc(ident_zeroed, 1)
                pool.wait_ge(ident_zeroed, 1)
                nc.gpsimd.affine_select(out=ident[:, :], in_=ident[:, :], compare_op=ALU.not_equal,
                                        fill=1.0, base=0, pattern=[[-1, P]],
                                        channel_multiplier=1).then_inc(ident_ready, 1)

                def load_part(t, c):
                    if CONVS * t + c >= 2:
                        pool.wait_ge(adj_used, CONVS * t + c - 1)
                    pool.dma_start(adj_part[c % 2][:, :],
                                   adj[t * P:(t + 1) * P, c * CONV:(c + 1) * CONV]).then_inc(early_adj_in[c % 2], 16)

                for c in range(2):
                    load_part(0, c)
                for t in range(2):
                    if t > 0:
                        pool.wait_ge(mask_ready, t)
                    pool.dma_start(adj_diag[:, :], adj[t * P:(t + 1) * P, t * P:(t + 1) * P]).then_inc(early_diag_in, 16)

                    def load_next(c, t=t):
                        if c + 2 < CONVS:
                            load_part(t, c + 2)
                        elif t == 0:
                            load_part(1, c + 2 - CONVS)
                    convert_tile(pool, (None,) * 4, 0, t, t, load_next)

            @block.sync
            def _(sp):
                def load_x(b, par):
                    sp.dma_start(x_rows[par][:, :, :], token_block(x, b)).then_inc(x_in[par], 16)

                for rows, w in zip(w_rows, (Wk, Wq, Wv)):
                    sp.dma_start(rows[:, :, :], w.rearrange("(f p) d -> p f d", p=P)).then_inc(w_in, 16)
                load_x(0, 0)
                with nc.allow_non_contiguous_dma(reason="two columns of biases"):
                    sp.dma_start(bias_k[:, :], bk.rearrange("(f p) -> p f", p=P)).then_inc(bias_in, 16)
                    sp.dma_start(bias_q[:, :], bq.rearrange("(f p) -> p f", p=P)).then_inc(bias_in, 16)
                for s in range(2):
                    sp.dma_start(bias_v[:, s, :], bv.partition_broadcast(P)).then_inc(bias_in, 16)
                load_x(1, 1)
                low_next = expected(sp)

                def pair(i, last):
                    plain = isinstance(i, int)
                    for par in range(2):
                        if not last:
                            sp.wait_ge(x_turned, 4 * i + 2 * par + 2)
                            load_x(2 * i + 2 + par, par)
                        for o in range(1 - par, 4):
                            step = 2 if par == 1 and o == 3 else 1
                            if plain:
                                sp.wait_ge(low_ready, 8 * i + 4 * par + o + 1)
                            elif o <= 2:
                                wait_then_add(sp, low_ready, low_next, step)
                            else:
                                sp.wait_ge(low_ready, low_next)
                            if o == 0:
                                for r in range(STACK):
                                    for h in range(GROUP):
                                        sp.dma_start(
                                            k_stack[h][r * DK:(r + 1) * DK, ds(2 * i * BANK, 2 * BANK)].bitcast(fp32),
                                            direct[h * DK:(h + 1) * DK, K_HALF[r], :].bitcast(fp32)
                                        ).then_inc(direct_stored, 16)
                            else:
                                dst, g = (k_halves, q_halves)[o // KB], o % KB
                                sp.dma_start(
                                    dst[:, g * P:(g + 1) * P, ds((2 * i + par) * BANK, BANK)].rearrange("r p n -> p r n"),
                                    halves[par][o - 1][:, :, :].bitcast(fp32)).then_inc(halves_stored[par], 16)
                            if not plain and o > 2:
                                sp.reg_alu(low_next, low_next, step, ALU.add)

                pair(0, False)
                sp.reg_mov(low_next, 8 + 2)
                with sp.Fori(1, PAIRS - 1) as i:
                    pair(i, False)
                sp.wait_ge(halves_stored[0], 16 * STORES)
                for tile in range(2):
                    load_q(sp, 0, tile, tile)
                pair(PAIRS - 1, True)
                sp.wait_ge(direct_stored, 16 * DIRECT * PAIRS)
                for par in range(2):
                    sp.wait_ge(halves_stored[par], PAIRS * STORES * 16)

            @block.tensor
            def _(pe):
                pe.wait_ge(ident_ready, 1)
                pe.wait_ge(w_in, 48)
                for w in range(3):
                    if w == 2:
                        pe.wait_ge(w_copied, 1)
                    for c in range(KB):
                        for f in range(KB):
                            last = nc.tensor.transpose(w_ps[w % 2][:, c * D + f * P:c * D + (f + 1) * P],
                                                       w_rows[w][:, f, c * P:(c + 1) * P], ident[:, :])
                    last.then_inc(w_turned, 1)
                pe.wait_ge(w_copied, 3)

                def pair(i):
                    for par in range(2):
                        pe.wait_ge(x_in[par], 16 * i + 16)
                        wait_reused(pe, x_copied, 4 * i + 2 * par)
                        for c in range(KB):
                            for s in range(SUB):
                                last = nc.tensor.transpose(x_ps[c][:, s * P:(s + 1) * P],
                                                           x_rows[par][:, s, c * P:(c + 1) * P], ident[:, :])
                            last.then_inc(x_turned, 1)
                        pe.wait_ge(x_copied, 4 * i + 2 * par + 2)
                        for o in range(4):
                            w, f = o // KB, o % KB
                            n = 8 * i + 4 * par + o
                            wait_reused(pe, low_ready, n - 1)
                            for c in range(KB):
                                last = nc.tensor.matmul(qk_ps[o % 2][:, :], w_cols[w][:, c, f * P:(f + 1) * P],
                                                        x_cols[par][:, c, :], start=(c == 0), stop=(c == KB - 1))
                            last.then_inc(qk_done, 1)
                        for k in range(2):
                            wait_reused(pe, v_ready, 4 * i + 2 * par)
                            for s in range(2):
                                for c in range(KB):
                                    last = nc.tensor.matmul(
                                        v_ps[k][:, s * D:(s + 1) * D],
                                        x_cols[par][:, c, (2 * k + s) * P:(2 * k + s + 1) * P],
                                        w_cols[2][:, c, :], start=(c == 0), stop=(c == KB - 1))
                            last.then_inc(v_done, 1)

                pairwise(pe, pair)

            @block.scalar
            def _(act):
                for w in range(3):
                    act.wait_ge(w_turned, w + 1)
                    nc.scalar.activation(w_cols[w][:, :, :].rearrange("p c n -> p (c n)"), w_ps[w % 2][:, :],
                                         ACT.Copy).then_inc(w_copied, 1)
                act.wait_ge(bias_in, 64)
                def pair(i):
                    for par in range(2):
                        wait_reused(act, v_done, 4 * i + 2 * par - 2)
                        for c in range(KB):
                            act.wait_ge(x_turned, 4 * i + 2 * par + c + 1)
                            nc.scalar.activation(x_cols[par][:, c, :], x_ps[c][:, :], ACT.Copy).then_inc(x_copied, 1)
                        for o in range(4):
                            wait_stored(act, i, par, o)
                            bias = (bias_k, bias_q)[o // KB]
                            act.wait_ge(qk_done, 8 * i + 4 * par + o + 1)
                            nc.scalar.activation(half(par, o, 0), qk_ps[o % 2][:, :], ACT.Identity,
                                                 bias=bias[:, o % KB:o % KB + 1]).then_inc(high_ready, 1)

                pairwise(act, pair)

            @block.vector
            def _(dve):
                dve.wait_ge(ident_ready, 1)
                nc.vector.tensor_copy(ident_i[:, :], ident[:, :]).then_inc(diag_step, 1)
                dve.wait_ge(bias_in, 64)
                def pair(i):
                    for par in range(2):
                        for o in range(4):
                            wait_stored(dve, i, par, o)
                            bias = (bias_k, bias_q)[o // KB]
                            dve.wait_ge(high_ready, 8 * i + 4 * par + o + 1)
                            nc.vector.scalar_tensor_tensor(
                                out=half(par, o, 1), in0=qk_ps[o % 2][:, :], scalar=bias[:, o % KB:o % KB + 1],
                                in1=half(par, o, 0).bitcast(fp32), op0=ALU.add,
                                op1=ALU.subtract).then_inc(low_ready, 1)
                        for k in range(2):
                            dve.wait_ge(v_done, 4 * i + 2 * par + k + 1)
                            nc.vector.tensor_tensor(
                                v_sb[:, ds((2 * i + par) * SUB + 2 * k, 2), :],
                                v_ps[k][:, :].rearrange("p (s n) -> p s n", s=2), bias_v[:, :, :],
                                ALU.add).then_inc(v_ready, 1)

                pairwise(dve, pair)

        with ExitStack() as stage:
            sb, bank, sem = allocators(stage)
            SCORES, TURNS = 2, 4
            UNITS = TILES * HEADS
            STEPS = 8

            exps = [sb(f"exps{i}", [P, N]) for i in range(4)]
            turned_sb = [sb(f"turned_sb{i}", [P, BANK]) for i in range(CHUNKS)]
            part_max = sb("part_max", [P, 2, CHUNKS])
            row_max = sb("row_max", [P, 2])
            neg_max = sb("neg_max", [P, 4])
            half_sums = sb("half_sums", [P, 4, 2])
            row_sum = sb("row_sum", [P, 4])
            inv_sum = sb("inv_sum", [P, 4])
            fold = sb("fold", [P, DK])
            ctx_cols = sb("ctx_cols", [P, P])
            ctx_rows = [sb(f"ctx_rows{i}", [P, P]) for i in range(2)]

            score_ps = [bank(f"score_ps{i}") for i in range(SCORES)]
            turn_ps = [bank(f"turn_ps{i}") for i in range(TURNS)]
            ctx_ps = [bank(f"ctx_ps{i}") for i in range(2)]

            k_in = [sem(f"k_in{h}") for h in range(GROUP)]
            scored = sem("scored")
            max_found = sem("max_found")
            max_ready = sem("max_ready")
            exped = sem("exped")
            turned = sem("turned")
            act_copied = sem("act_copied")
            dve_copied = sem("dve_copied")
            weighed = sem("weighed")
            ctx_copied = sem("ctx_copied")
            folded = sem("folded")
            sum_found = sem("sum_found")
            inv_ready = sem("inv_ready")
            normed = sem("normed")
            ctx_stored = [sem(f"ctx_stored{i}") for i in range(2)]
            fold_made = sem("fold_made")

            BURST = 2
            BEHIND = 4
            DVE_GROUPS = (0, 4)
            ACT_GROUPS = tuple(c for c in range(CHUNKS) if c not in DVE_GROUPS)

            def wait_copied(eng, unit, c):
                if c in DVE_GROUPS:
                    eng.wait_ge(dve_copied, len(DVE_GROUPS) * unit + DVE_GROUPS.index(c) + 1)
                else:
                    eng.wait_ge(act_copied, len(ACT_GROUPS) * unit + ACT_GROUPS.index(c) + 1)

            def every_step(eng, step, ahead_of_loop=None):
                for u in range(2):
                    step(u, u, u)
                half = UNITS // GROUPS
                for g in range(GROUPS):
                    first = 2 if g == 0 else g * half + 2
                    for u in range(first, first + STEPS - 2 if g == 0 else first + 6):
                        step(u, u % STEPS, u)
                    start = g * half + STEPS
                    if ahead_of_loop:
                        ahead_of_loop(start)
                    with eng.Fori(0, (half - STEPS) // STEPS) as i:
                        for j in range(STEPS):
                            step(start + STEPS * i + j, j, None)
                    if g < GROUPS - 1:
                        for u in range((g + 1) * half, (g + 1) * half + 2):
                            step(u, u % STEPS, u)
                for u in range(UNITS, UNITS + 5):
                    step(u, u % STEPS, u)

            def has(u, lag):
                return not isinstance(u, int) or 0 <= u - lag < UNITS

            def group_of(n, lag):
                return 0 if n - lag < UNITS // GROUPS else 1

            block = stage.enter_context(nc.Block())

            @block.sync
            def _(sp):
                def load_k(g, heads):
                    for h in heads:
                        sp.wait_ge(scored, CHUNKS * (g * UNITS // GROUPS - GROUP + h + 1))
                        rows = ds((g * GROUP + h) * DK, DK)
                        for r in range(STACK):
                            sp.dma_start(k_stack[h][r * DK:(r + 1) * DK, :].bitcast(fp32),
                                         k_halves[K_HALF[r], rows, :]).then_inc(k_in[h], 16)

                adj_used_next = expected(sp)

                def load_tile(g, tg, par, half_way=None):
                    t = g * TILES + tg
                    sp.wait_ge(scored, CHUNKS * GROUP * (t - 1))
                    load_q(sp, g, tg, par)
                    sp.wait_ge(mask_ready, t)
                    sp.dma_start(adj_diag[:, :], adj[ds(tg * P, P), ds(tg * P, P)]).then_inc(diag_in, 16)
                    for c in range(CONVS):
                        if c == CONVS // 2 and half_way:
                            half_way()
                        if not isinstance(t, int):
                            wait_then_add(sp, adj_used, adj_used_next, 1)
                        elif t > 0 or c >= 2:
                            sp.wait_ge(adj_used, CONVS * t + c - 1)
                        sp.dma_start(adj_part[c % 2][:, :],
                                     adj[ds(tg * P, P), c * CONV:(c + 1) * CONV]).then_inc(adj_in[c % 2], 16)

                for g in range(GROUPS):
                    if g > 0:
                        load_tile(g, 0, 0, lambda: load_k(g, range(1)))
                        load_k(g, range(1, GROUP))
                        load_tile(g, 1, 1)
                    sp.reg_mov(adj_used_next, CONVS * (g * TILES + 2) - 1)
                    with sp.Fori(1, TILES // 2) as i:
                        for par in range(2):
                            load_tile(g, 2 * i + par, par)

                sp.wait_ge(scored, CHUNKS * (UNITS - GROUP + 1))
                sp.dma_start(w1_rows[:, :, :], W1.rearrange("(f p) d -> p f d", p=P)).then_inc(wts_in, 16)
                sp.dma_start(w2_rows[:, :, :], W2.rearrange("(f p) d -> p f d", p=P)).then_inc(wts_in, 16)
                sp.wait_ge(scored, CHUNKS * (UNITS - GROUP + 2))
                sp.dma_start(wo_rows[:, :, :], Wo.rearrange("(f p) d -> p f d", p=P)).then_inc(wts_in, 16)
                for par in range(2):
                    sp.wait_ge(ctx_stored[0], 16 * ((GROUPS - 1) * TILES // 2 + SUB))
                    sp.wait_ge(ctx_stored[1], 16 * ((GROUPS - 1) * TILES // 2 + SUB))
                    sp.dma_start(ctx_in_sb[par][:, :, :], token_block(ctx_dram, par)).then_inc(ctx_in[par], 16)
                for k, a in row_names.items():
                    sp.dma_start(rows_of[k][:, :], a.partition_broadcast(P)).then_inc(rows_in, 16)
                sp.wait_ge(scored, CHUNKS * (UNITS - GROUP + 3))
                for par in range(2):
                    sp.dma_start(x_in_sb[par][:, :, :], token_block(x, par)).then_inc(xr_in[par], 16)
                with nc.allow_non_contiguous_dma(reason="eight columns of biases"):
                    sp.dma_start(b1_cols[:, :], b1.rearrange("(f p) -> p f", p=P)).then_inc(rows_in, 16)

            @block.gpsimd
            def _(pool):
                counts = mask_counts(pool)
                for g in range(GROUPS):
                    if g > 0:
                        for par in range(2):
                            convert_tile(pool, counts, g, par, par)
                    set_mask_counts(pool, counts, g * TILES + 2)
                    with pool.Fori(1, TILES // 2) as i:
                        for par in range(2):
                            convert_tile(pool, counts, g, 2 * i + par, par)

            @block.tensor
            def _(pe):
                def step(u, m, n):
                    h = m % GROUP
                    par = m // GROUP
                    for burst in range(CHUNKS // BURST):
                        chunks = range(burst * BURST, (burst + 1) * BURST)
                        if has(u, 2):
                            for c in chunks:
                                turn(u - 2, m, n, c)
                        if has(u, 0):
                            if burst == 0 and h == 0:
                                pe.wait_ge(q_in[par], 8 * (u - m) + 16 * STACK)
                            if burst == 0 and n is not None and n > GROUP and n % (UNITS // GROUPS) < GROUP:
                                pe.wait_ge(k_in[h], 16 * STACK * group_of(n, 0))
                            for c in chunks:
                                if n is None or n > 0 or c >= SCORES:
                                    pe.wait_ge(masked, CHUNKS * u + c - SCORES + 1)
                                nc.tensor.matmul(score_ps[c % SCORES][:, :], q_stack[par][:, h, :],
                                                 k_stack[h][:, c * BANK:(c + 1) * BANK],
                                                 start=True, stop=True).then_inc(scored, 1)
                        if chunks[0] == BEHIND + 2 and has(u, 3):
                            v = u - 3
                            pe.wait_ge(ctx_copied, v + 1)
                            nc.tensor.matmul(ctx_ps[(m - 3) % 2][:, P:P + DK], ctx_cols[:, :], fold[:, :],
                                             start=True, stop=True).then_inc(folded, 1)
                        for c in chunks:
                            if c < BEHIND and has(u, 3):
                                weigh(u - 3, m, n, 3, c + CHUNKS - BEHIND)
                            elif c >= BEHIND and has(u, 2):
                                weigh(u - 2, m, n, 2, c - BEHIND)

                def turn(v, m, n, c):
                    if c % (CHUNKS // 2) == 0:
                        pe.wait_ge(exped, 2 * v + c // (CHUNKS // 2) + 1)
                    if c >= TURNS:
                        wait_copied(pe, v, c - TURNS)
                    elif n is None or n > 2:
                        wait_copied(pe, v - 1, c + CHUNKS - TURNS)
                    for j in range(SUB):
                        kt = c * SUB + j
                        last = nc.tensor.transpose(turn_ps[c % TURNS][:, j * P:(j + 1) * P],
                                                   exps[(m - 2) % 4][:, kt * P:(kt + 1) * P], ident[:, :])
                    last.then_inc(turned, 1)

                def weigh(v, m, n, lag, c):
                    wait_copied(pe, v, c)
                    if c == 0 and (n is None or n > 3):
                        pe.wait_ge(normed, v - 1)
                    head, side = (m - lag) % GROUP, (m - lag) % 2
                    for j in range(SUB):
                        last = nc.tensor.matmul(
                            ctx_ps[side][j * DK:(j + 1) * DK, 0:P], v_heads(n, lag, c * SUB + j, head),
                            turned_sb[c][:, j * P:(j + 1) * P],
                            start=(c == 0), stop=(c == CHUNKS - 1), tile_position=(0, j * DK))
                    last.then_inc(weighed, 1)

                loop_group = [0]

                def v_heads(n, lag, kt, head):
                    g = group_of(n, lag) if n is not None else loop_group[0]
                    f = (g * GROUP + head) * DK
                    return v_sb[:, kt, f:f + DK]

                def counted(u, m, n):
                    if n is not None:
                        loop_group[0] = group_of(n, 0)
                    step(u, m, n)

                pe.wait_ge(fold_made, GROUP)
                every_step(pe, counted)

            @block.scalar
            def _(act):
                def step(u, m, n):
                    for half in range(2):
                        if has(u, 1):
                            v, b = u - 1, (m - 1) % 4
                            if half == 0:
                                act.wait_ge(max_ready, v + 1)
                            cols = slice(half * N // 2, (half + 1) * N // 2)
                            nc.scalar.activation(exps[b][:, cols], exps[b][:, cols], ACT.Exp,
                                                 bias=neg_max[:, b:b + 1], scale=SCALE,
                                                 accum_out=half_sums[:, b, half:half + 1]).then_inc(exped, 1)
                        if has(u, 2):
                            v = u - 2
                            for c in ACT_GROUPS:
                                if c // (CHUNKS // 2) != half:
                                    continue
                                act.wait_ge(turned, CHUNKS * v + c + 1)
                                if n is None or n > 2:
                                    act.wait_ge(weighed, CHUNKS * (v - 1) + c + 1)
                                nc.scalar.activation(turned_sb[c][:, :], turn_ps[c % TURNS][:, :],
                                                     ACT.Copy).then_inc(act_copied, 1)
                        if half == 0 and m % GROUP == 0 and (n is None or n >= 8):
                            act.wait_ge(normed, u - 4)
                            store(u - 8, n, (m % STEPS) // GROUP)

                def store(v, n, par):
                    g = group_of(n, 8) if n is not None else loop_group[0]
                    row = (v - g * (UNITS // GROUPS)) * (P // GROUP)
                    act.dma_start(ctx_dram[ds(row, P), g * P:(g + 1) * P],
                                  ctx_rows[par][:, :]).then_inc(ctx_stored[par], 16)

                loop_group = [0]

                def counted(u, m, n):
                    if n is not None:
                        loop_group[0] = group_of(n, 0)
                    step(u, m, n)

                every_step(act, counted)
                for par in range(2):
                    act.wait_ge(ctx_stored[par], 16 * TILES * GROUPS // 2)

            @block.vector
            def _(dve):
                for j in range(GROUP):
                    nc.vector.tensor_copy(fold[j * DK:(j + 1) * DK, :],
                                          ident[j * DK:(j + 1) * DK, j * DK:(j + 1) * DK]).then_inc(fold_made, 1)
                scored_next = expected(dve)

                def step(u, m, n):
                    h, par = m % GROUP, m // GROUP
                    for c in range(CHUNKS):
                        if has(u, 0):
                            if c == 0:
                                if h == 0:
                                    dve.wait_ge(mask_ready, tile_count(u - m, par))
                                if n is None or n >= 4:
                                    dve.wait_ge(turned, CHUNKS * (u - 3))
                            if n is None:
                                wait_then_add(dve, scored, scored_next, 1)
                            else:
                                dve.wait_ge(scored, CHUNKS * u + c + 1)
                            cols = slice(c * BANK, (c + 1) * BANK)
                            nc.vector.tensor_tensor_reduce(
                                out=exps[m % 4][:, cols], in0=score_ps[c % SCORES][:, :], in1=mask[par][:, cols],
                                scale=1.0, scalar=LOWEST, op0=ALU.add, op1=ALU.max,
                                accum_out=part_max[:, m % 2, c:c + 1]).then_inc(masked, 1)
                        if c - 1 in DVE_GROUPS and has(u, 2):
                            v = u - 2
                            dve.wait_ge(turned, CHUNKS * v + c)
                            if n is None or n > 2:
                                dve.wait_ge(weighed, CHUNKS * (v - 1) + c)
                            nc.vector.tensor_copy(turned_sb[c - 1][:, :],
                                                  turn_ps[(c - 1) % TURNS][:, :]).then_inc(dve_copied, 1)
                        if c == 1 and has(u, 2):
                            v, b = u - 2, (m - 2) % 4
                            dve.wait_ge(exped, 2 * v + 2)
                            nc.vector.tensor_tensor(row_sum[:, b:b + 1], half_sums[:, b, 0:1],
                                                    half_sums[:, b, 1:2], ALU.add).then_inc(sum_found, 1)
                        if c == 3 and has(u, 2):
                            v, b = u - 2, (m - 2) % 4
                            dve.wait_ge(sum_found, v + 1)
                            nc.vector.reciprocal(inv_sum[:, b:b + 1], row_sum[:, b:b + 1]).then_inc(inv_ready, 1)
                        if c == BEHIND and has(u, 3):
                            v, side = u - 3, (m - 3) % 2
                            dve.wait_ge(weighed, CHUNKS * (v + 1))
                            if n is None or n > 3:
                                dve.wait_ge(folded, v)
                            nc.vector.tensor_copy(ctx_cols[:, :], ctx_ps[side][:, 0:P]).then_inc(ctx_copied, 1)
                    if has(u, 0):
                        dve.wait_ge(masked, CHUNKS * u + CHUNKS)
                        nc.vector.reduce_max(row_max[:, m % 2:m % 2 + 1], part_max[:, m % 2, :],
                                             AX.X).then_inc(max_found, 1)
                        dve.wait_ge(max_found, u + 1)
                        nc.vector.tensor_scalar(neg_max[:, m % 4:m % 4 + 1], row_max[:, m % 2:m % 2 + 1], -SCALE,
                                                None, ALU.mult).then_inc(max_ready, 1)
                    if has(u, 3):
                        v, b = u - 3, (m - 3) % 4
                        tile_par = ((m - 3) % STEPS) // GROUP
                        dve.wait_ge(folded, v + 1)
                        dve.wait_ge(inv_ready, v + 1)
                        if b == 0 and (n is None or n > 8):
                            dve.wait_ge(ctx_stored[tile_par], 2 * (v - (m - 3) % STEPS))
                        nc.vector.tensor_scalar(ctx_rows[tile_par][:, b * DK:(b + 1) * DK], ctx_ps[(m - 3) % 2][:, P:P + DK],
                                                inv_sum[:, b:b + 1], None, ALU.mult).then_inc(normed, 1)

                def tile_count(first, par):
                    if isinstance(first, int):
                        return first // GROUP + par + 1
                    return tiles_before[0] + par + 1

                tiles_before = [0]

                def counted(u, m, n):
                    if n is None:
                        tiles_before[0] = (u - m) // GROUP
                    step(u, m, n)

                every_step(dve, counted, lambda start: dve.reg_mov(scored_next, CHUNKS * start + 1))

        with ExitStack() as stage:
            sb, bank, sem = allocators(stage)
            wo_cols = sb("wo_cols", [P, KB, D])
            w1_cols = sb("w1_cols", [P, KB, FF])
            w2_cols = sb("w2_cols", [P, FB, D])
            ctx_t = sb("ctx_t", [P, KB, BANK])
            h1 = [sb(f"h1_{i}", [P, SUB, D]) for i in range(2)]
            h1_t = [sb(f"h1_t{i}", [P, KB, BANK]) for i in range(2)]
            hidden = sb("hidden", [P, FB, BANK])
            pre = [sb(f"pre{i}", [P, SUB, D]) for i in range(2)]
            stats = [sb(f"stats{i}", [P, SUB, 6]) for i in range(2)]
            mean_var = [sb(f"mean_var{i}", [P, SUB, 2]) for i in range(2)]
            var_eps = [sb(f"var_eps{i}", [P, SUB]) for i in range(2)]
            idle = sb("idle", [P, 1])
            std = [sb(f"std{i}", [P, SUB]) for i in range(2)]
            std_inv = [sb(f"std_inv{i}", [P, SUB]) for i in range(2)]
            newton = [sb(f"newton{i}", [P, SUB]) for i in range(2)]
            final = [sb(f"final{i}", [P, SUB, D]) for i in range(2)]
            turn_ps = [bank(f"c_turn_ps{i}") for i in range(2)]
            wo_ps = [bank(f"wo_ps{i}") for i in range(2)]
            up_ps = [bank(f"up_ps{i}") for i in range(2)]
            down_ps = [bank(f"down_ps{i}") for i in range(2)]

            wt_turned = sem("wt_turned")
            wt_copied = sem("wt_copied")
            ctx_turned = sem("ctx_turned")
            ctx_copied = sem("ctx_copied_c")
            h1_turned = sem("h1_turned")
            h1_copied = sem("h1_copied")
            wo_done = sem("wo_done")
            wo_read = sem("wo_read")
            h1_ready = sem("h1_ready")
            up_done = sem("up_done")
            up_read = sem("up_read")
            down_done = sem("down_done")
            down_read = sem("down_read")
            ln_step = sem("ln_step")
            std_ready = sem("std_ready")
            final_ready = sem("final_ready")
            out_stored = [sem(f"out_stored{i}") for i in range(2)]
            PAIRS = BLOCKS // 2
            other_banks = up_ps + down_ps

            block = stage.enter_context(nc.Block())

            @block.sync
            def _(sp):
                def load(b, par):
                    sp.wait_ge(wo_read, 2 * b - 2)
                    sp.dma_start(ctx_in_sb[par][:, :, :], token_block(ctx_dram, b)).then_inc(ctx_in[par], 16)
                    sp.dma_start(x_in_sb[par][:, :, :], token_block(x, b)).then_inc(xr_in[par], 16)

                def store(b, par):
                    sp.wait_ge(final_ready, b + 1)
                    sp.dma_start(token_block(out, b), final[par][:, :, :]).then_inc(out_stored[par], 16)

                with sp.Fori(0, PAIRS - 1) as i:
                    for par in range(2):
                        load(2 * i + 2 + par, par)
                        store(2 * i + par, par)
                for par in range(2):
                    store(BLOCKS - 2 + par, par)
                for par in range(2):
                    sp.wait_ge(out_stored[par], 16 * PAIRS)

            NORM = 2 + 16

            def ln1_before(b):
                return NORM * (2 * b - 1)

            def ln2_before(b, last_block):
                return NORM * (2 * b + (1 if last_block else 2))

            def blockwise(eng, step):
                for b in range(3):
                    step(b, b % 2, b == 0, False)
                with eng.Fori(0, (BLOCKS - 4) // 2) as i:
                    for j in range(2):
                        step(2 * i + 3 + j, (3 + j) % 2, False, False)
                step(BLOCKS - 1, 1, False, True)

            @block.tensor
            def _(pe):
                pe.wait_ge(wts_in, 48)

                def turn_pair(rows, f0, bank):
                    for c in range(KB):
                        for f in range(2):
                            last = nc.tensor.transpose(bank[:, (2 * c + f) * P:(2 * c + f + 1) * P],
                                                       rows[:, f0 + f, c * P:(c + 1) * P], ident[:, :])
                    last.then_inc(wt_turned, 1)

                def turn_ctx(b, par, first):
                    pe.wait_ge(ctx_in[par], 8 * (b - par) + 16)
                    for c in range(KB):
                        if not first:
                            pe.wait_ge(wo_read, 2 * b)
                        for s in range(SUB):
                            last = nc.tensor.transpose(wo_ps[c][:, s * P:(s + 1) * P],
                                                       ctx_in_sb[par][:, s, c * P:(c + 1) * P], ident[:, :])
                        last.then_inc(ctx_turned, 1)

                def project(b):
                    pe.wait_ge(ctx_copied, 2 * b + 2)
                    for k in range(2):
                        for s in range(2):
                            for c in range(KB):
                                last = nc.tensor.matmul(wo_ps[k][:, s * D:(s + 1) * D],
                                                        ctx_t[:, c, (2 * k + s) * P:(2 * k + s + 1) * P],
                                                        wo_cols[:, c, :], start=(c == 0), stop=(c == KB - 1))
                        last.then_inc(wo_done, 1)

                def turn_h1(b, par):
                    pe.wait_ge(h1_ready, b + 1)
                    for c in range(KB):
                        for s in range(SUB):
                            last = nc.tensor.transpose(turn_ps[c][:, s * P:(s + 1) * P],
                                                       h1[par][:, s, c * P:(c + 1) * P], ident[:, :])
                        last.then_inc(h1_turned, 1)

                def up(b, par, first):
                    pe.wait_ge(h1_copied, 2 * b + 2)
                    for m in range(FB):
                        if not (first and m < 2):
                            pe.wait_ge(up_read, FB * b + m - 1)
                        for c in range(KB):
                            last = nc.tensor.matmul(up_ps[m % 2][:, :], w1_cols[:, c, m * P:(m + 1) * P],
                                                    h1_t[par][:, c, :], start=(c == 0), stop=(c == KB - 1))
                        last.then_inc(up_done, 1)

                def down(b, first):
                    pe.wait_ge(up_read, FB * b + FB)
                    for k in range(2):
                        if not first:
                            pe.wait_ge(down_read, 2 * b)
                        for s in range(2):
                            for m in range(FB):
                                last = nc.tensor.matmul(down_ps[k][:, s * D:(s + 1) * D],
                                                        hidden[:, m, (2 * k + s) * P:(2 * k + s + 1) * P],
                                                        w2_cols[:, m, :], start=(m == 0), stop=(m == FB - 1))
                        last.then_inc(down_done, 1)

                turn_pair(wo_rows, 0, turn_ps[0])
                turn_ctx(0, 0, True)
                pe.wait_ge(wt_copied, 1)
                project(0)
                for n, (f0, bank) in enumerate(zip(range(0, FB, 2), other_banks)):
                    turn_pair(w1_rows, f0, bank)
                for n, (m0, bank) in enumerate(zip(range(0, FB, 2), other_banks)):
                    pe.wait_ge(wt_copied, 1 + n + 1)
                    for m in range(2):
                        for f in range(KB):
                            last = nc.tensor.transpose(bank[:, (2 * m + f) * P:(2 * m + f + 1) * P],
                                                       w2_rows[:, f, (m0 + m) * P:(m0 + m + 1) * P], ident[:, :])
                    last.then_inc(wt_turned, 1)
                turn_ctx(1, 1, False)
                project(1)
                turn_h1(0, 0)
                pe.wait_ge(wt_copied, 1 + 2 * len(other_banks))

                def step(b, par, first, last):
                    if not (first or last):
                        turn_ctx(b + 1, 1 - par, False)
                    up(b, par, first)
                    if not (first or last):
                        project(b + 1)
                    down(b, first)
                    if not last:
                        turn_h1(b + 1, 1 - par)

                blockwise(pe, step)

            @block.scalar
            def _(act):
                def copy_pair(n, cols, f0, bank):
                    act.wait_ge(wt_turned, n)
                    nc.scalar.activation(cols[:, :, f0 * P:(f0 + 2) * P],
                                         bank[:, :].rearrange("p (c n) -> p c n", c=KB),
                                         ACT.Copy).then_inc(wt_copied, 1)

                def ctx_copy(b, first):
                    for c in range(KB):
                        act.wait_ge(ctx_turned, 2 * b + c + 1)
                        if not first:
                            act.wait_ge(wo_done, 2 * b)
                        nc.scalar.activation(ctx_t[:, c, :], wo_ps[c][:, :], ACT.Copy).then_inc(ctx_copied, 1)

                def h1_copy(b, par, early):
                    for c in range(KB):
                        act.wait_ge(h1_turned, 2 * b + c + 1)
                        if not early:
                            act.wait_ge(up_done, FB * (b - 1))
                        nc.scalar.activation(h1_t[par][:, c, :], turn_ps[c][:, :], ACT.Copy).then_inc(h1_copied, 1)

                def root(w, before):
                    act.wait_ge(ln_step, before + 11)
                    nc.scalar.activation(std[w][:, :], var_eps[w][:, :], ACT.Sqrt).then_inc(std_ready, 1)

                copy_pair(1, wo_cols, 0, turn_ps[0])
                ctx_copy(0, True)
                act.wait_ge(rows_in, 16 * (len(row_names) + 1))
                for n, bank in enumerate(other_banks):
                    copy_pair(2 + n, w1_cols, 2 * n, bank)
                for n, bank in enumerate(other_banks):
                    act.wait_ge(wt_turned, 2 + len(other_banks) + n)
                    nc.scalar.activation(w2_cols[:, 2 * n:2 * n + 2, :],
                                         bank[:, :].rearrange("p (m n) -> p m n", m=2),
                                         ACT.Copy).then_inc(wt_copied, 1)
                ctx_copy(1, False)
                root(0, 0)
                h1_copy(0, 0, True)

                def step(b, par, first, last):
                    if not (first or last):
                        ctx_copy(b + 1, False)
                    for m in range(FB):
                        if m == 2 and not first:
                            root(1, ln2_before(b - 1, False))
                        act.wait_ge(up_done, FB * b + m + 1)
                        if not first:
                            act.wait_ge(down_done, 2 * b)
                        nc.scalar.activation(hidden[:, m, :], up_ps[m % 2][:, :], ACT.Relu,
                                             bias=b1_cols[:, m:m + 1]).then_inc(up_read, 1)
                    if not last:
                        root(0, ln1_before(b + 1))
                        h1_copy(b + 1, 1 - par, first)

                blockwise(act, step)
                root(1, ln2_before(BLOCKS - 1, True))

            @block.vector
            def _(dve):
                def norm(w, done, which, gain, shift, to, end):
                    for s in range(SUB):
                        nc.vector.bn_stats(stats[w][:, s, :], pre[w][:, s, :]).then_inc(ln_step, 1)
                    dve.wait_ge(ln_step, done + 4)
                    nc.vector.memset(idle[:, :], 0.0)
                    for s in range(SUB):
                        nc.vector.bn_aggr(mean_var[w][:, s, :], stats[w][:, s, :]).then_inc(ln_step, 1)
                    dve.wait_ge(ln_step, done + 8)
                    nc.vector.tensor_scalar(var_eps[w][:, :], mean_var[w][:, :, 1], EPS, None,
                                            ALU.add).then_inc(ln_step, 1)
                    dve.wait_ge(std_ready, which + 1)
                    nc.vector.reciprocal(std_inv[w][:, :], std[w][:, :]).then_inc(ln_step, 1)
                    dve.wait_ge(ln_step, done + 10)
                    nc.vector.tensor_tensor(newton[w][:, :], std_inv[w][:, :], std_inv[w][:, :],
                                            ALU.mult).then_inc(ln_step, 1)
                    dve.wait_ge(ln_step, done + 11)
                    nc.vector.tensor_tensor(newton[w][:, :], newton[w][:, :], var_eps[w][:, :],
                                            ALU.mult).then_inc(ln_step, 1)
                    dve.wait_ge(ln_step, done + 12)
                    nc.vector.tensor_scalar(newton[w][:, :], newton[w][:, :], -0.5, 1.5, ALU.mult,
                                            ALU.add).then_inc(ln_step, 1)
                    dve.wait_ge(ln_step, done + 13)
                    nc.vector.tensor_tensor(std_inv[w][:, :], std_inv[w][:, :], newton[w][:, :],
                                            ALU.mult).then_inc(ln_step, 1)
                    dve.wait_ge(ln_step, done + 14)
                    for s in range(SUB):
                        last = nc.vector.tensor_scalar(to[:, s, :], pre[w][:, s, :], mean_var[w][:, s, 0:1],
                                                       std_inv[w][:, s:s + 1], ALU.subtract, ALU.mult)
                    last.then_inc(ln_step, 1)
                    dve.wait_ge(ln_step, done + 15)
                    for s in range(SUB):
                        last = nc.vector.tensor_tensor(to[:, s, :], to[:, s, :], rows_of[gain][:, :], ALU.mult)
                    last.then_inc(ln_step, 1)
                    dve.wait_ge(ln_step, done + 16)
                    for s in range(SUB):
                        last = nc.vector.tensor_tensor(to[:, s, :], to[:, s, :], rows_of[shift][:, :], ALU.add)
                    last.then_inc(end, 1)

                def ln1(b, par, early):
                    done = 0 if early else ln1_before(b)
                    dve.wait_ge(xr_in[par], 8 * (b - par) + 16)
                    for k in range(2):
                        dve.wait_ge(wo_done, 2 * b + k + 1)
                        for s in range(2):
                            last = nc.vector.tensor_tensor(pre[0][:, 2 * k + s, :], wo_ps[k][:, s * D:(s + 1) * D],
                                                           rows_of["bo"][:, :], ALU.add)
                        last.then_inc(ln_step, 1)
                    dve.wait_ge(ln_step, done + 2)
                    for k in range(2):
                        last = nc.vector.tensor_tensor(pre[0][:, 2 * k:2 * k + 2, :], pre[0][:, 2 * k:2 * k + 2, :],
                                                       x_in_sb[par][:, 2 * k:2 * k + 2, :], ALU.add)
                        last.then_inc(wo_read, 1)
                    dve.wait_ge(wo_read, 2 * b + 2)
                    norm(0, done + 2, 0 if early else 2 * b - 1, "g1", "s1", h1[par], h1_ready)

                def ln2(b, par, early, last_block):
                    done = ln2_before(b, last_block)
                    dve.wait_ge(h1_ready, b + 1)
                    for k in range(2):
                        dve.wait_ge(down_done, 2 * b + k + 1)
                        for s in range(2):
                            last = nc.vector.tensor_tensor(pre[1][:, 2 * k + s, :], down_ps[k][:, s * D:(s + 1) * D],
                                                           rows_of["b2"][:, :], ALU.add)
                        last.then_inc(ln_step, 1)
                    dve.wait_ge(ln_step, done + 2)
                    for k in range(2):
                        last = nc.vector.tensor_tensor(pre[1][:, 2 * k:2 * k + 2, :], pre[1][:, 2 * k:2 * k + 2, :],
                                                       h1[par][:, 2 * k:2 * k + 2, :], ALU.add)
                        last.then_inc(down_read, 1)
                    dve.wait_ge(down_read, 2 * b + 2)
                    if not early:
                        dve.wait_ge(out_stored[par], 8 * (b - par))
                    norm(1, done + 2, 2 * b + (1 if last_block else 2), "g2", "s2", final[par], final_ready)

                dve.wait_ge(rows_in, 16 * (len(row_names) + 1))
                ln1(0, 0, True)

                def step(b, par, first, last):
                    if not first:
                        ln2(b - 1, 1 - par, isinstance(b, int) and b < 3, False)
                    if not last:
                        ln1(b + 1, 1 - par, False)

                blockwise(dve, step)
                ln2(BLOCKS - 1, 1, False, True)


_INS = ["x", "adj", "L0_gnn_Wq", "L0_gnn_bq", "L0_gnn_Wk", "L0_gnn_bk", "L0_gnn_Wv", "L0_gnn_bv", "L0_gnn_Wo",
        "L0_gnn_bo", "L0_gnn_W1", "L0_gnn_b1", "L0_gnn_W2", "L0_gnn_b2", "L0_gnn_ln1_g", "L0_gnn_ln1_b",
        "L0_gnn_ln2_g", "L0_gnn_ln2_b"]


def kernel(**inputs):
    import numpy as _np
    import concourse.bacc as _bacc
    from concourse import mybir as _mybir
    from concourse.bass_utils import run_bass_kernel_spmd as _run

    nc = _bacc.Bacc("TRN2", target_bir_lowering=False, num_devices=1)
    arrays, args = {}, []
    for name in _INS:
        a = _np.ascontiguousarray(inputs[name])
        arrays[f"in_{name}"] = a
        args.append(nc.dram_tensor(f"in_{name}", a.shape, _mybir.dt.from_np(a.dtype), kind="ExternalInput").ap())
    out = nc.dram_tensor("out_h2", inputs["x"].shape, _mybir.dt.float32, kind="ExternalOutput").ap()
    build_gnn_layer(nc, *args, out)
    r = _run(nc, [arrays], core_ids=[0])
    return r.results[0]["out_h2"]
```

```python
import concourse.bass as bass
from concourse import mybir
from contextlib import ExitStack


def build_gnn_layer(nc, x, adj, Wq, bq, Wk, bk, Wv, bv, Wo, bo, W1, b1, W2, b2,
                    ln1_g, ln1_b, ln2_g, ln2_b, out):
    fp32, fp32r, bf16, i32 = (mybir.dt.float32, mybir.dt.float32r, mybir.dt.bfloat16, mybir.dt.int32)
    ALU, ACT, AX = mybir.AluOpType, mybir.ActivationFunctionType, mybir.AxisListType
    ds = bass.ds

    N, D = x.shape
    FF = W1.shape[0]
    P = 128
    BANK = 512
    HEADS, DK = 8, 32
    GROUP = P // DK
    GROUPS = HEADS // GROUP
    STACK = 4
    K_HALF = (0, 1, 0, 1)
    Q_HALF = (0, 0, 1, 1)
    KB = D // P
    FB = FF // P
    TILES = N // P
    SUB = BANK // P
    BLOCKS = N // BANK
    SCALE = float(DK) ** -0.5
    MASKED = -1.0e9 / SCALE
    LOWEST = -3.0e38
    CHUNKS = N // BANK
    CONV = BANK
    CONVS = N // CONV
    PAIRED = 2
    EARLY = 2 * PAIRED
    STEP_CHUNKS = PAIRED * CHUNKS
    EPS = 1e-5

    k_halves = nc.dram_tensor("k_halves", (2, D, N), fp32, kind="Internal").ap()
    q_halves = nc.dram_tensor("q_halves", (2, D, N), fp32, kind="Internal").ap()
    v_late = nc.dram_tensor("v_late", (N, P), fp32, kind="Internal").ap()
    ctx_dram = nc.dram_tensor("ctx_rows", (N, D), fp32, kind="Internal").ap()

    def expected(eng):
        register = eng.alloc_register()
        eng.reg_mov(register, 0)
        return register

    def wait_then_add(eng, semaphore, register, step):
        eng.wait_ge(semaphore, register)
        eng.reg_alu(register, register, step, ALU.add)

    def allocators(stack):
        def sb(name, shape, dt=fp32):
            return stack.enter_context(nc.sbuf_tensor(name, shape, dt))

        def bank(name):
            return stack.enter_context(nc.psum_tensor(name, [P, BANK], fp32))

        def sem(name):
            return stack.enter_context(nc.semaphore(name))
        return sb, bank, sem

    def token_block(a, b):
        return a[ds(b * BANK, BANK), :].rearrange("(s p) d -> p s d", p=P)

    whole = ExitStack()
    with whole:
        sb, bank, sem = allocators(whole)
        ident = sb("ident", [P, P])
        v_sb = sb("v_sb", [P, TILES, P])

        row_names = {"bo": bo, "b2": b2, "g1": ln1_g, "s1": ln1_b, "g2": ln2_g, "s2": ln2_b}
        with ExitStack() as shared:
            sb, _, _ = allocators(shared)
            w1_rows = sb("w1_rows", [P, FB, D])
            w2_rows = sb("w2_rows", [P, KB, FF])
            wo_rows = sb("wo_rows", [P, KB, D])
            rows_of = {k: sb(f"row_{k}", [P, D]) for k in row_names}
            ctx_in_sb = [sb(f"ctx_in_sb{i}", [P, SUB, D]) for i in range(2)]
            x_in_sb = [sb(f"x_in_sb{i}", [P, SUB, D]) for i in range(2)]
            b1_cols = sb("b1_cols", [P, FB])
        sb, bank, sem = allocators(whole)
        k_stack = [sb(f"k_stack{h}", [P, N], fp32r) for h in range(GROUP)]
        q_stack = [sb(f"q_stack{i}", [P, GROUP, P], fp32r) for i in range(2 * PAIRED)]
        mask = [sb(f"mask{i}", [P, N], bf16) for i in range(2 * PAIRED)]
        adj_part = [sb(f"adj_part{i}", [P, CONV], i32) for i in range(2)]
        adj_diag = sb("adj_diag", [P, P], i32)
        mask_diag = sb("mask_diag", [P, P], bf16)
        q_in = [sem(f"q_in{i}") for i in range(2 * PAIRED)]
        adj_in = [sem(f"adj_in{i}") for i in range(2)]
        diag_in = sem("diag_in")
        early_adj_in = [sem(f"early_adj_in{i}") for i in range(2)]
        early_diag_in = sem("early_diag_in")
        adj_used = sem("adj_used")
        diag_step = sem("diag_step")
        mask_ready = sem("mask_ready")
        masked = sem("masked")
        wts_in = sem("wts_in")
        rows_in = sem("rows_in")
        ctx_in = [sem(f"ctx_in{i}") for i in range(2)]
        xr_in = [sem(f"xr_in{i}") for i in range(2)]

        def load_q(sp, g, tg, buf):
            for r in range(STACK):
                src = q_halves[Q_HALF[r], g * P:(g + 1) * P, ds(tg * P, P)].rearrange("(h d) n -> d h n", d=DK)
                sp.dma_start(q_stack[buf][r * DK:(r + 1) * DK, :, :].bitcast(fp32), src).then_inc(q_in[buf], 16)

        def mask_counts(pool):
            return expected(pool), expected(pool), *([expected(pool) for _ in range(2)] for _ in range(2))

        def set_mask_counts(pool, counts, t):
            turned_next, ready_next, masked_next, adj_in_next = counts
            pool.reg_mov(ready_next, t)
            pool.reg_mov(turned_next, 3 * t + 1)
            for k in range(2):
                pool.reg_mov(masked_next[k], last_use(t) + k + 1)
                pool.reg_mov(adj_in_next[k], 16 * (CONVS // 2) * (t - PAIRED) + 16)

        def convert_tile(pool, counts, g, tg, buf, after_part=None):
            step_next, ready_next, masked_next, adj_in_next = counts
            t = g * TILES + tg
            side = buf % PAIRED
            diag, part, before = (early_diag_in, early_adj_in, 0) if after_part else (diag_in, adj_in, PAIRED)
            looped = not isinstance(t, int)
            pool.wait_ge(diag, 16 * (t - before) + 16)
            if looped:
                wait_then_add(pool, mask_ready, ready_next, 1)
            elif t > 0:
                pool.wait_ge(mask_ready, t)
            nc.gpsimd.tensor_scalar(mask_diag[:, :], adj_diag[:, :], 0.0, MASKED, ALU.is_equal,
                                    ALU.mult).then_inc(diag_step, 1)
            if looped:
                wait_then_add(pool, diag_step, step_next, 3)
            else:
                pool.wait_ge(diag_step, 3 * t + 1)
            nc.gpsimd.affine_select(out=mask_diag[:, :], in_=mask_diag[:, :], compare_op=ALU.not_equal,
                                    fill=0.0, base=0, pattern=[[-1, P]],
                                    channel_multiplier=1).then_inc(diag_step, 1)
            for c in range(CONVS):
                if looped:
                    wait_then_add(pool, adj_in[c % 2], adj_in_next[c % 2], 16)
                    wait_then_add(pool, masked, masked_next[side],
                                  PAIRED if c < CONVS - 1 else STEP_CHUNKS * GROUP - (CONVS - 1) * PAIRED)
                else:
                    pool.wait_ge(part[c % 2], 16 * (CONVS // 2) * (t - before) + 16 * (c // 2) + 16)
                    if t >= EARLY:
                        pool.wait_ge(masked, last_use(t - side) + c * PAIRED + side + 1)
                nc.gpsimd.tensor_scalar(mask[buf][:, c * CONV:(c + 1) * CONV], adj_part[c % 2][:, :],
                                        0.0, MASKED, ALU.is_equal, ALU.mult).then_inc(adj_used, 1)
                if after_part:
                    after_part(c)
            pool.wait_ge(adj_used, CONVS * t + CONVS)
            pool.wait_ge(diag_step, 3 * t + 2)
            nc.gpsimd.tensor_copy(mask[buf][:, ds(tg * P, P)], mask_diag[:, :]).then_inc(diag_step, 1)
            pool.wait_ge(diag_step, 3 * t + 3)
            pool.sem_inc(mask_ready, 1)

        def last_use(t):
            return STEP_CHUNKS * (GROUP * (t // PAIRED - 1) - 1)

        with ExitStack() as stage:
            sb, bank, sem = allocators(stage)
            w_rows = [sb(f"w_rows{w}", [P, KB, D]) for w in range(3)]
            w_cols = [sb(f"w_cols{w}", [P, KB, D]) for w in range(3)]
            bias_k = sb("bias_k", [P, KB])
            bias_q = sb("bias_q", [P, KB])
            bias_v = sb("bias_v", [P, 2, D])
            x_rows = [sb(f"x_rows{i}", [P, SUB, D]) for i in range(2)]
            x_cols = [sb(f"x_cols{i}", [P, KB, BANK]) for i in range(2)]
            halves = [[sb(f"halves{i}_{o}", [P, 2, BANK], fp32r) for o in range(1, 4)] for i in range(2)]
            v_staged = sb("v_staged", [P, TILES, P])
            direct = sb("direct", [P, 2, 2 * BANK], fp32r)
            w_ps = [bank(f"w_ps{i}") for i in range(2)]
            x_ps = [bank(f"x_ps{i}") for i in range(2)]
            qk_ps = [bank(f"qk_ps{i}") for i in range(2)]
            v_ps = [bank(f"v_ps{i}") for i in range(2)]

            w_in = sem("w_in")
            bias_in = sem("bias_in")
            ident_zeroed = sem("ident_zeroed")
            ident_ready = sem("ident_ready")
            w_turned = sem("w_turned")
            w_copied = sem("w_copied")
            x_in = [sem(f"x_in{i}") for i in range(2)]
            x_turned = sem("x_turned")
            x_copied = sem("x_copied")
            qk_done = sem("qk_done")
            high_ready = sem("high_ready")
            low_ready = sem("low_ready")
            halves_stored = [sem(f"halves_stored{i}") for i in range(2)]
            direct_stored = sem("direct_stored")
            v_stored = sem("v_stored")
            v_done = sem("v_done")
            v_ready = sem("v_ready")
            PAIRS = BLOCKS // 2
            STORES = 3
            DIRECT = STACK * GROUP

            def half(par, o, which):
                if o == 0:
                    return direct[:, which, par * BANK:(par + 1) * BANK]
                return halves[par][o - 1][:, which, :]

            def pairwise(eng, pair):
                pair(0)
                with eng.Fori(1, PAIRS) as i:
                    pair(i)

            def wait_reused(eng, semaphore, value):
                if not isinstance(value, int) or value > 0:
                    eng.wait_ge(semaphore, value)

            def wait_stored(eng, i, par, o):
                if o == 0 and par == 0:
                    wait_reused(eng, direct_stored, 16 * DIRECT * i)
                elif o == 1:
                    wait_reused(eng, halves_stored[par], 16 * STORES * i)

            block = stage.enter_context(nc.Block())

            @block.gpsimd
            def _(pool):
                nc.gpsimd.memset(ident[:, :], 0.0).then_inc(ident_zeroed, 1)
                pool.wait_ge(ident_zeroed, 1)
                nc.gpsimd.affine_select(out=ident[:, :], in_=ident[:, :], compare_op=ALU.not_equal,
                                        fill=1.0, base=0, pattern=[[-1, P]],
                                        channel_multiplier=1).then_inc(ident_ready, 1)

                def load_part(t, c):
                    if CONVS * t + c >= 2:
                        pool.wait_ge(adj_used, CONVS * t + c - 1)
                    pool.dma_start(adj_part[c % 2][:, :],
                                   adj[t * P:(t + 1) * P, c * CONV:(c + 1) * CONV]).then_inc(early_adj_in[c % 2], 16)

                for c in range(2):
                    load_part(0, c)
                for t in range(PAIRED):
                    if t > 0:
                        pool.wait_ge(mask_ready, t)
                    pool.dma_start(adj_diag[:, :], adj[t * P:(t + 1) * P, t * P:(t + 1) * P]).then_inc(early_diag_in, 16)

                    def load_next(c, t=t):
                        if c + 2 < CONVS:
                            load_part(t, c + 2)
                        elif t + 1 < PAIRED:
                            load_part(t + 1, c + 2 - CONVS)
                    convert_tile(pool, (None,) * 4, 0, t, t, load_next)

                for b in range(BLOCKS):
                    pool.wait_ge(v_ready, 2 * b + 2)
                    pool.dma_start(v_late[b * BANK:(b + 1) * BANK, :].rearrange("(s p) d -> p s d", p=P),
                                   v_staged[:, b * SUB:(b + 1) * SUB, :]).then_inc(v_stored, 16)
                pool.wait_ge(v_stored, 16 * BLOCKS)

            @block.sync
            def _(sp):
                def load_x(b, par):
                    sp.dma_start(x_rows[par][:, :, :], token_block(x, b)).then_inc(x_in[par], 16)

                for rows, w in zip(w_rows, (Wk, Wq, Wv)):
                    sp.dma_start(rows[:, :, :], w.rearrange("(f p) d -> p f d", p=P)).then_inc(w_in, 16)
                load_x(0, 0)
                with nc.allow_non_contiguous_dma(reason="two columns of biases"):
                    sp.dma_start(bias_k[:, :], bk.rearrange("(f p) -> p f", p=P)).then_inc(bias_in, 16)
                    sp.dma_start(bias_q[:, :], bq.rearrange("(f p) -> p f", p=P)).then_inc(bias_in, 16)
                for s in range(2):
                    sp.dma_start(bias_v[:, s, :], bv.partition_broadcast(P)).then_inc(bias_in, 16)
                load_x(1, 1)
                low_next = expected(sp)

                def pair(i, last):
                    plain = isinstance(i, int)
                    for par in range(2):
                        if not last:
                            sp.wait_ge(x_turned, 4 * i + 2 * par + 2)
                            load_x(2 * i + 2 + par, par)
                        for o in range(1 - par, 4):
                            step = 2 if par == 1 and o == 3 else 1
                            if plain:
                                sp.wait_ge(low_ready, 8 * i + 4 * par + o + 1)
                            elif o <= 2:
                                wait_then_add(sp, low_ready, low_next, step)
                            else:
                                sp.wait_ge(low_ready, low_next)
                            if o == 0:
                                for r in range(STACK):
                                    for h in range(GROUP):
                                        sp.dma_start(
                                            k_stack[h][r * DK:(r + 1) * DK, ds(2 * i * BANK, 2 * BANK)].bitcast(fp32),
                                            direct[h * DK:(h + 1) * DK, K_HALF[r], :].bitcast(fp32)
                                        ).then_inc(direct_stored, 16)
                            else:
                                dst, g = (k_halves, q_halves)[o // KB], o % KB
                                sp.dma_start(
                                    dst[:, g * P:(g + 1) * P, ds((2 * i + par) * BANK, BANK)].rearrange("r p n -> p r n"),
                                    halves[par][o - 1][:, :, :].bitcast(fp32)).then_inc(halves_stored[par], 16)
                            if not plain and o > 2:
                                sp.reg_alu(low_next, low_next, step, ALU.add)

                pair(0, False)
                sp.reg_mov(low_next, 8 + 2)
                with sp.Fori(1, PAIRS - 1) as i:
                    pair(i, False)
                sp.wait_ge(halves_stored[0], 16 * STORES)
                for tile in range(EARLY):
                    load_q(sp, 0, tile, tile)
                pair(PAIRS - 1, True)
                sp.wait_ge(direct_stored, 16 * DIRECT * PAIRS)
                for par in range(2):
                    sp.wait_ge(halves_stored[par], PAIRS * STORES * 16)

            @block.tensor
            def _(pe):
                pe.wait_ge(ident_ready, 1)
                pe.wait_ge(w_in, 48)
                for w in range(3):
                    if w == 2:
                        pe.wait_ge(w_copied, 1)
                    for c in range(KB):
                        for f in range(KB):
                            last = nc.tensor.transpose(w_ps[w % 2][:, c * D + f * P:c * D + (f + 1) * P],
                                                       w_rows[w][:, f, c * P:(c + 1) * P], ident[:, :])
                    last.then_inc(w_turned, 1)
                pe.wait_ge(w_copied, 3)

                def pair(i):
                    for par in range(2):
                        pe.wait_ge(x_in[par], 16 * i + 16)
                        wait_reused(pe, x_copied, 4 * i + 2 * par)
                        for c in range(KB):
                            for s in range(SUB):
                                last = nc.tensor.transpose(x_ps[c][:, s * P:(s + 1) * P],
                                                           x_rows[par][:, s, c * P:(c + 1) * P], ident[:, :])
                            last.then_inc(x_turned, 1)
                        pe.wait_ge(x_copied, 4 * i + 2 * par + 2)
                        for o in range(4):
                            w, f = o // KB, o % KB
                            n = 8 * i + 4 * par + o
                            wait_reused(pe, low_ready, n - 1)
                            for c in range(KB):
                                last = nc.tensor.matmul(qk_ps[o % 2][:, :], w_cols[w][:, c, f * P:(f + 1) * P],
                                                        x_cols[par][:, c, :], start=(c == 0), stop=(c == KB - 1))
                            last.then_inc(qk_done, 1)
                        for k in range(2):
                            wait_reused(pe, v_ready, 4 * i + 2 * par)
                            for s in range(2):
                                for c in range(KB):
                                    last = nc.tensor.matmul(
                                        v_ps[k][:, s * D:(s + 1) * D],
                                        x_cols[par][:, c, (2 * k + s) * P:(2 * k + s + 1) * P],
                                        w_cols[2][:, c, :], start=(c == 0), stop=(c == KB - 1))
                            last.then_inc(v_done, 1)

                pairwise(pe, pair)

            @block.scalar
            def _(act):
                for w in range(3):
                    act.wait_ge(w_turned, w + 1)
                    nc.scalar.activation(w_cols[w][:, :, :].rearrange("p c n -> p (c n)"), w_ps[w % 2][:, :],
                                         ACT.Copy).then_inc(w_copied, 1)
                act.wait_ge(bias_in, 64)
                def pair(i):
                    for par in range(2):
                        wait_reused(act, v_done, 4 * i + 2 * par - 2)
                        for c in range(KB):
                            act.wait_ge(x_turned, 4 * i + 2 * par + c + 1)
                            nc.scalar.activation(x_cols[par][:, c, :], x_ps[c][:, :], ACT.Copy).then_inc(x_copied, 1)
                        for o in range(4):
                            wait_stored(act, i, par, o)
                            bias = (bias_k, bias_q)[o // KB]
                            act.wait_ge(qk_done, 8 * i + 4 * par + o + 1)
                            nc.scalar.activation(half(par, o, 0), qk_ps[o % 2][:, :], ACT.Identity,
                                                 bias=bias[:, o % KB:o % KB + 1]).then_inc(high_ready, 1)

                pairwise(act, pair)

            @block.vector
            def _(dve):
                dve.wait_ge(bias_in, 64)
                def pair(i):
                    for par in range(2):
                        for o in range(4):
                            wait_stored(dve, i, par, o)
                            bias = (bias_k, bias_q)[o // KB]
                            dve.wait_ge(high_ready, 8 * i + 4 * par + o + 1)
                            nc.vector.scalar_tensor_tensor(
                                out=half(par, o, 1), in0=qk_ps[o % 2][:, :], scalar=bias[:, o % KB:o % KB + 1],
                                in1=half(par, o, 0).bitcast(fp32), op0=ALU.add,
                                op1=ALU.subtract).then_inc(low_ready, 1)
                        for k in range(2):
                            dve.wait_ge(v_done, 4 * i + 2 * par + k + 1)
                            for g, to in enumerate((v_sb, v_staged)):
                                last = nc.vector.tensor_tensor(
                                    to[:, ds((2 * i + par) * SUB + 2 * k, 2), :],
                                    v_ps[k][:, :].rearrange("p (s n) -> p s n", s=2)[:, :, g * P:(g + 1) * P],
                                    bias_v[:, :, g * P:(g + 1) * P], ALU.add)
                            last.then_inc(v_ready, 1)

                pairwise(dve, pair)

        with ExitStack() as stage:
            sb, bank, sem = allocators(stage)
            TURNS = 4
            UNITS = TILES * HEADS // PAIRED
            HALF_UNITS = UNITS // GROUPS
            STEPS = 2 * GROUP
            BEHIND = 2

            exps = [[sb(f"exps{i}_{s}", [P, N]) for s in range(PAIRED)] for i in range(2)]
            turned_sb = [sb(f"turned_sb{i}", [P, SUB, PAIRED, P]) for i in range(TURNS)]
            part_max = sb("part_max", [P, 2, PAIRED, CHUNKS])
            row_max = sb("row_max", [P, 2, PAIRED])
            neg_max = sb("neg_max", [P, 2, PAIRED])
            half_sums = sb("half_sums", [P, 2, 2, PAIRED])
            row_sum = sb("row_sum", [P, 2, PAIRED])
            inv_sum = sb("inv_sum", [P, 2, PAIRED])
            fold = sb("fold", [P, DK])
            ctx_cols = sb("ctx_cols", [P, PAIRED * P])
            ctx_rows = [sb(f"ctx_rows{s}", [P, P]) for s in range(PAIRED)]

            score_ps = [bank(f"score_ps{s}") for s in range(PAIRED)]
            turn_ps = [bank(f"turn_ps{i}") for i in range(TURNS)]
            ctx_ps = [bank(f"ctx_ps{i}") for i in range(2)]

            k_in = [sem(f"k_in{h}") for h in range(GROUP)]
            v_in = [sem(f"v_in{c}") for c in range(CHUNKS)]
            scored = sem("scored")
            max_found = sem("max_found")
            max_ready = sem("max_ready")
            exped = sem("exped")
            turned = sem("turned")
            act_copied = sem("act_copied")
            dve_copied = sem("dve_copied")
            weighed = sem("weighed")
            ctx_copied = sem("ctx_copied")
            folded = sem("folded")
            sum_found = sem("sum_found")
            inv_ready = sem("inv_ready")
            normed = sem("normed")
            ctx_stored = sem("ctx_stored")
            fold_made = sem("fold_made")

            def by_dve(c, s):
                return c % 2 == 1 and s == 1

            def wait_copied(eng, unit, c, s):
                if by_dve(c, s):
                    eng.wait_ge(dve_copied, CHUNKS // 2 * unit + c // 2 + 1)
                else:
                    eng.wait_ge(act_copied, 3 * CHUNKS // 2 * unit + 3 * (c // 2) + 2 * (c % 2) + s + 1)

            def every_step(eng, step, ahead_of_loop=None):
                for g in range(GROUPS):
                    start = g * HALF_UNITS + STEPS
                    for u in range(g * HALF_UNITS, start):
                        step(u, u % STEPS, u)
                    if ahead_of_loop:
                        ahead_of_loop(start)
                    with eng.Fori(0, (HALF_UNITS - STEPS) // STEPS) as i:
                        for j in range(STEPS):
                            step(start + STEPS * i + j, j, None)
                for u in range(UNITS, UNITS + GROUP):
                    step(u, u % STEPS, u)

            def has(u, lag):
                return not isinstance(u, int) or 0 <= u - lag < UNITS

            block = stage.enter_context(nc.Block())

            @block.sync
            def _(sp):
                def load_k(g, h):
                    sp.wait_ge(scored, STEP_CHUNKS * (g * HALF_UNITS - GROUP + h + 1))
                    rows = ds((g * GROUP + h) * DK, DK)
                    for r in range(STACK):
                        sp.dma_start(k_stack[h][r * DK:(r + 1) * DK, :].bitcast(fp32),
                                     k_halves[K_HALF[r], rows, :]).then_inc(k_in[h], 16)

                def load_v(g, c):
                    sp.wait_ge(weighed, CHUNKS * (g * HALF_UNITS - 1) + c + 1)
                    sp.dma_start(v_sb[:, c * SUB:(c + 1) * SUB, :],
                                 v_late[c * BANK:(c + 1) * BANK, :].rearrange("(s p) d -> p s d", p=P)
                                 ).then_inc(v_in[c], 16)

                adj_used_next = expected(sp)

                def load_tile(g, pair, buf):
                    side = buf % PAIRED
                    tg = PAIRED * pair + side
                    t = g * TILES + tg
                    if isinstance(t, int) and t < EARLY:
                        pass
                    else:
                        sp.wait_ge(scored, STEP_CHUNKS * GROUP * (g * TILES // PAIRED + pair - 1))
                        load_q(sp, g, tg, buf)
                    sp.wait_ge(mask_ready, t)
                    sp.dma_start(adj_diag[:, :], adj[ds(tg * P, P), ds(tg * P, P)]).then_inc(diag_in, 16)
                    for c in range(CONVS):
                        if isinstance(t, int):
                            sp.wait_ge(adj_used, CONVS * t + c - 1)
                        else:
                            wait_then_add(sp, adj_used, adj_used_next, 1)
                        sp.dma_start(adj_part[c % 2][:, :],
                                     adj[ds(tg * P, P), c * CONV:(c + 1) * CONV]).then_inc(adj_in[c % 2], 16)

                for g in range(GROUPS):
                    if g == 0:
                        for s in range(PAIRED):
                            load_tile(0, 1, PAIRED + s)
                    else:
                        load_tile(g, 0, 0)
                        load_k(g, 0)
                        load_tile(g, 0, 1)
                        for h in range(1, GROUP):
                            load_k(g, h)
                        load_tile(g, 1, 2)
                        for c in range(CHUNKS):
                            load_v(g, c)
                        load_tile(g, 1, 3)
                    sp.reg_mov(adj_used_next, CONVS * (g * TILES + EARLY) - 1)
                    with sp.Fori(1, TILES // EARLY) as i:
                        for buf in range(EARLY):
                            load_tile(g, 2 * i + buf // PAIRED, buf)

                sp.wait_ge(scored, STEP_CHUNKS * (UNITS - GROUP + 1))
                sp.dma_start(w1_rows[:, :, :], W1.rearrange("(f p) d -> p f d", p=P)).then_inc(wts_in, 16)
                sp.dma_start(w2_rows[:, :, :], W2.rearrange("(f p) d -> p f d", p=P)).then_inc(wts_in, 16)
                sp.wait_ge(scored, STEP_CHUNKS * (UNITS - GROUP + 2))
                sp.dma_start(wo_rows[:, :, :], Wo.rearrange("(f p) d -> p f d", p=P)).then_inc(wts_in, 16)
                sp.wait_ge(ctx_stored, 16 * ((GROUPS - 1) * TILES + 2 * SUB))
                for par in range(2):
                    sp.dma_start(ctx_in_sb[par][:, :, :], token_block(ctx_dram, par)).then_inc(ctx_in[par], 16)
                for k, a in row_names.items():
                    sp.dma_start(rows_of[k][:, :], a.partition_broadcast(P)).then_inc(rows_in, 16)
                sp.wait_ge(scored, STEP_CHUNKS * (UNITS - GROUP + 3))
                for par in range(2):
                    sp.dma_start(x_in_sb[par][:, :, :], token_block(x, par)).then_inc(xr_in[par], 16)
                with nc.allow_non_contiguous_dma(reason="eight columns of biases"):
                    sp.dma_start(b1_cols[:, :], b1.rearrange("(f p) -> p f", p=P)).then_inc(rows_in, 16)

            @block.gpsimd
            def _(pool):
                counts = mask_counts(pool)
                for g in range(GROUPS):
                    for tile in range(PAIRED if g == 0 else 0, EARLY):
                        convert_tile(pool, counts, g, tile, tile)
                    set_mask_counts(pool, counts, g * TILES + EARLY)
                    with pool.Fori(1, TILES // EARLY) as i:
                        for buf in range(EARLY):
                            convert_tile(pool, counts, g, EARLY * i + buf, buf)

            @block.tensor
            def _(pe):
                def step(u, m, n):
                    h, pair_buf = m % GROUP, m // GROUP * PAIRED
                    for c in range(CHUNKS):
                        if has(u, 2):
                            for s in range(PAIRED):
                                turn(u - 2, m, n, c, s)
                        if has(u, 0):
                            if c == 0 and n is not None and HALF_UNITS <= n < HALF_UNITS + GROUP:
                                pe.wait_ge(k_in[h], 16 * STACK)
                            for s in range(PAIRED):
                                if c == 0 and h == 0:
                                    pe.wait_ge(q_in[pair_buf + s], 8 * (u - m) + 16 * STACK)
                                if n is None or n > 0 or c > 0:
                                    pe.wait_ge(masked, STEP_CHUNKS * u + PAIRED * c + s - 1)
                                nc.tensor.matmul(score_ps[s][:, :], q_stack[pair_buf + s][:, h, :],
                                                 k_stack[h][:, c * BANK:(c + 1) * BANK],
                                                 start=True, stop=True).then_inc(scored, 1)
                        if c == 2 * BEHIND and has(u, 3):
                            pe.wait_ge(ctx_copied, u - 2)
                            for s in range(PAIRED):
                                last = nc.tensor.matmul(
                                    ctx_ps[(m - 3) % 2][:, PAIRED * P + s * DK:PAIRED * P + (s + 1) * DK],
                                    ctx_cols[:, s * P:(s + 1) * P], fold[:, :], start=True, stop=True)
                            last.then_inc(folded, 1)
                        if c < BEHIND and has(u, 3):
                            weigh(u - 3, m, n, 3, c + CHUNKS - BEHIND)
                        elif c >= BEHIND and has(u, 2):
                            weigh(u - 2, m, n, 2, c - BEHIND)

                def turn(v, m, n, c, s):
                    if c % (CHUNKS // 2) == 0:
                        pe.wait_ge(exped, 4 * v + PAIRED * (c // (CHUNKS // 2)) + s + 1)
                    if c >= 2:
                        wait_copied(pe, v, c - 2, s)
                    elif n is None or n > 2:
                        wait_copied(pe, v - 1, c + CHUNKS - 2, s)
                    for j in range(SUB):
                        kt = c * SUB + j
                        last = nc.tensor.transpose(turn_ps[(PAIRED * c + s) % TURNS][:, j * P:(j + 1) * P],
                                                   exps[m % 2][s][:, kt * P:(kt + 1) * P], ident[:, :])
                    last.then_inc(turned, 1)

                def weigh(v, m, n, lag, c):
                    for s in range(PAIRED):
                        wait_copied(pe, v, c, s)
                    if c == 0 and (n is None or n > 3):
                        pe.wait_ge(normed, v - 1)
                    if n is not None and n - lag == HALF_UNITS:
                        pe.wait_ge(v_in[c], 16)
                    head, side = (m - lag) % GROUP, (m - lag) % 2
                    for j in range(SUB):
                        last = nc.tensor.matmul(
                            ctx_ps[side][j * DK:(j + 1) * DK, 0:PAIRED * P],
                            v_sb[:, c * SUB + j, head * DK:(head + 1) * DK],
                            turned_sb[c % TURNS][:, j, :, :].rearrange("p s n -> p (s n)"),
                            start=(c == 0), stop=(c == CHUNKS - 1), tile_position=(0, j * DK))
                    last.then_inc(weighed, 1)

                pe.wait_ge(fold_made, GROUP)
                every_step(pe, step)

            def copy_group(eng, copy, v, n, c, s):
                eng.wait_ge(turned, STEP_CHUNKS * v + PAIRED * c + s + 1)
                if n is None or n > 2 or c >= TURNS:
                    eng.wait_ge(weighed, CHUNKS * v + c - TURNS + 1)
                return copy(turned_sb[c % TURNS][:, :, s, :],
                            turn_ps[(PAIRED * c + s) % TURNS][:, :].rearrange("p (j n) -> p j n", j=SUB))

            @block.scalar
            def _(act):
                def step(u, m, n):
                    for quarter in range(4):
                        if has(u, 2):
                            for s in range(PAIRED):
                                act_copy(u - 2, n, 2 * quarter, s)
                        if has(u, 1):
                            v, b = u - 1, (m - 1) % 2
                            half, s = quarter // PAIRED, quarter % PAIRED
                            if quarter == 0:
                                act.wait_ge(max_ready, v + 1)
                            cols = slice(half * N // 2, (half + 1) * N // 2)
                            nc.scalar.activation(exps[b][s][:, cols], exps[b][s][:, cols], ACT.Exp,
                                                 bias=neg_max[:, b, s:s + 1], scale=SCALE,
                                                 accum_out=half_sums[:, b, half, s:s + 1]).then_inc(exped, 1)
                        if has(u, 2):
                            act_copy(u - 2, n, 2 * quarter + 1, 0)
                        if quarter == 0 and m % GROUP == 3 and (n is None or n >= 7):
                            act.wait_ge(normed, u - 3)
                            store(u - 7, n)

                def act_copy(v, n, c, s):
                    copy_group(act, lambda to, src: nc.scalar.activation(to, src, ACT.Copy),
                               v, n, c, s).then_inc(act_copied, 1)

                def store(v, n):
                    if n is not None:
                        loop_group[0] = v // HALF_UNITS
                    g = loop_group[0]
                    for s in range(PAIRED):
                        row = (v - g * HALF_UNITS) * (PAIRED * P // GROUP) + s * P
                        act.dma_start(ctx_dram[ds(row, P), g * P:(g + 1) * P],
                                      ctx_rows[s][:, :]).then_inc(ctx_stored, 16)

                loop_group = [0]

                def counted(u, m, n):
                    step(u, m, n)
                    if n is not None:
                        loop_group[0] = min(n // HALF_UNITS, GROUPS - 1)

                every_step(act, counted)
                act.wait_ge(ctx_stored, 16 * TILES * GROUPS)

            @block.vector
            def _(dve):
                for j in range(GROUP):
                    nc.vector.tensor_copy(fold[j * DK:(j + 1) * DK, :],
                                          ident[j * DK:(j + 1) * DK, j * DK:(j + 1) * DK]).then_inc(fold_made, 1)
                scored_next = expected(dve)

                def step(u, m, n):
                    h, pair_buf = m % GROUP, m // GROUP * PAIRED
                    for c in range(CHUNKS):
                        if has(u, 0):
                            if c == 0 and h == 0:
                                dve.wait_ge(mask_ready, pair_count(u - m, m // GROUP) * PAIRED)
                            for s in range(PAIRED):
                                if n is None:
                                    wait_then_add(dve, scored, scored_next, 1)
                                else:
                                    dve.wait_ge(scored, STEP_CHUNKS * u + PAIRED * c + s + 1)
                                cols = slice(c * BANK, (c + 1) * BANK)
                                nc.vector.tensor_tensor_reduce(
                                    out=exps[m % 2][s][:, cols], in0=score_ps[s][:, :],
                                    in1=mask[pair_buf + s][:, cols],
                                    scale=1.0, scalar=LOWEST, op0=ALU.add, op1=ALU.max,
                                    accum_out=part_max[:, m % 2, s, c:c + 1]).then_inc(masked, 1)
                        if c % 2 == 1 and has(u, 2):
                            copy_group(dve, nc.vector.tensor_copy, u - 2, n, c, 1).then_inc(dve_copied, 1)
                        if c == 0 and has(u, 2):
                            v, b = u - 2, m % 2
                            dve.wait_ge(exped, 4 * v + 4)
                            nc.vector.tensor_tensor(row_sum[:, b, :], half_sums[:, b, 0, :],
                                                    half_sums[:, b, 1, :], ALU.add).then_inc(sum_found, 1)
                        if c == 4 and has(u, 2):
                            v, b = u - 2, m % 2
                            dve.wait_ge(sum_found, v + 1)
                            nc.vector.reciprocal(inv_sum[:, b, :], row_sum[:, b, :]).then_inc(inv_ready, 1)
                        if c == BEHIND and has(u, 3):
                            v = u - 3
                            dve.wait_ge(weighed, CHUNKS * (v + 1))
                            if n is None or n > 3:
                                dve.wait_ge(folded, v)
                            nc.vector.tensor_copy(ctx_cols[:, :],
                                                  ctx_ps[(m - 3) % 2][:, 0:PAIRED * P]).then_inc(ctx_copied, 1)
                        if c == 6 and has(u, 3):
                            v, b, head = u - 3, (m - 3) % 2, (m - 3) % GROUP
                            dve.wait_ge(folded, v + 1)
                            dve.wait_ge(inv_ready, v + 1)
                            if head == 0 and (n is None or n > 3):
                                dve.wait_ge(ctx_stored, 16 * PAIRED // GROUP * v)
                            for s in range(PAIRED):
                                last = nc.vector.tensor_scalar(
                                    ctx_rows[s][:, head * DK:(head + 1) * DK],
                                    ctx_ps[b][:, PAIRED * P + s * DK:PAIRED * P + (s + 1) * DK],
                                    inv_sum[:, b, s:s + 1], None, ALU.mult)
                            last.then_inc(normed, 1)
                    if has(u, 0):
                        b = m % 2
                        dve.wait_ge(masked, STEP_CHUNKS * u + STEP_CHUNKS)
                        nc.vector.reduce_max(row_max[:, b, :], part_max[:, b, :, :],
                                             AX.X).then_inc(max_found, 1)
                        dve.wait_ge(max_found, u + 1)
                        nc.vector.tensor_scalar(neg_max[:, b, :], row_max[:, b, :], -SCALE,
                                                None, ALU.mult).then_inc(max_ready, 1)

                def pair_count(first, second):
                    return first // GROUP + second + 1

                every_step(dve, step, lambda start: dve.reg_mov(scored_next, STEP_CHUNKS * start + 1))

        with ExitStack() as stage:
            sb, bank, sem = allocators(stage)
            wo_cols = sb("wo_cols", [P, KB, D])
            w1_cols = sb("w1_cols", [P, KB, FF])
            w2_cols = sb("w2_cols", [P, FB, D])
            ctx_t = sb("ctx_t", [P, KB, BANK])
            h1 = [sb(f"h1_{i}", [P, SUB, D]) for i in range(2)]
            h1_t = [sb(f"h1_t{i}", [P, KB, BANK]) for i in range(2)]
            hidden = sb("hidden", [P, FB, BANK])
            pre = [sb(f"pre{i}", [P, SUB, D]) for i in range(2)]
            stats = [sb(f"stats{i}", [P, SUB, 6]) for i in range(2)]
            mean_var = [sb(f"mean_var{i}", [P, SUB, 2]) for i in range(2)]
            var_eps = [sb(f"var_eps{i}", [P, SUB]) for i in range(2)]
            idle = sb("idle", [P, 1])
            std = [sb(f"std{i}", [P, SUB]) for i in range(2)]
            std_inv = [sb(f"std_inv{i}", [P, SUB]) for i in range(2)]
            newton = [sb(f"newton{i}", [P, SUB]) for i in range(2)]
            final = [sb(f"final{i}", [P, SUB, D]) for i in range(2)]
            turn_ps = [bank(f"c_turn_ps{i}") for i in range(2)]
            wo_ps = [bank(f"wo_ps{i}") for i in range(2)]
            up_ps = [bank(f"up_ps{i}") for i in range(2)]
            down_ps = [bank(f"down_ps{i}") for i in range(2)]

            wt_turned = sem("wt_turned")
            wt_copied = sem("wt_copied")
            ctx_turned = sem("ctx_turned")
            ctx_copied = sem("ctx_copied_c")
            h1_turned = sem("h1_turned")
            h1_copied = sem("h1_copied")
            wo_done = sem("wo_done")
            wo_read = sem("wo_read")
            h1_ready = sem("h1_ready")
            up_done = sem("up_done")
            up_read = sem("up_read")
            down_done = sem("down_done")
            down_read = sem("down_read")
            ln_step = sem("ln_step")
            std_ready = sem("std_ready")
            final_ready = sem("final_ready")
            out_stored = [sem(f"out_stored{i}") for i in range(2)]
            PAIRS = BLOCKS // 2
            other_banks = up_ps + down_ps

            block = stage.enter_context(nc.Block())

            @block.sync
            def _(sp):
                def load(b, par):
                    sp.wait_ge(wo_read, 2 * b - 2)
                    sp.dma_start(ctx_in_sb[par][:, :, :], token_block(ctx_dram, b)).then_inc(ctx_in[par], 16)
                    sp.dma_start(x_in_sb[par][:, :, :], token_block(x, b)).then_inc(xr_in[par], 16)

                def store(b, par):
                    sp.wait_ge(final_ready, b + 1)
                    sp.dma_start(token_block(out, b), final[par][:, :, :]).then_inc(out_stored[par], 16)

                with sp.Fori(0, PAIRS - 1) as i:
                    for par in range(2):
                        load(2 * i + 2 + par, par)
                        store(2 * i + par, par)
                for par in range(2):
                    store(BLOCKS - 2 + par, par)
                for par in range(2):
                    sp.wait_ge(out_stored[par], 16 * PAIRS)

            NORM = 2 + 16

            def ln1_before(b):
                return NORM * (2 * b - 1)

            def ln2_before(b, last_block):
                return NORM * (2 * b + (1 if last_block else 2))

            def blockwise(eng, step):
                for b in range(3):
                    step(b, b % 2, b == 0, False)
                with eng.Fori(0, (BLOCKS - 4) // 2) as i:
                    for j in range(2):
                        step(2 * i + 3 + j, (3 + j) % 2, False, False)
                step(BLOCKS - 1, 1, False, True)

            @block.tensor
            def _(pe):
                pe.wait_ge(wts_in, 48)

                def turn_pair(rows, f0, bank):
                    for c in range(KB):
                        for f in range(2):
                            last = nc.tensor.transpose(bank[:, (2 * c + f) * P:(2 * c + f + 1) * P],
                                                       rows[:, f0 + f, c * P:(c + 1) * P], ident[:, :])
                    last.then_inc(wt_turned, 1)

                def turn_ctx(b, par, first):
                    pe.wait_ge(ctx_in[par], 8 * (b - par) + 16)
                    for c in range(KB):
                        if not first:
                            pe.wait_ge(wo_read, 2 * b)
                        for s in range(SUB):
                            last = nc.tensor.transpose(wo_ps[c][:, s * P:(s + 1) * P],
                                                       ctx_in_sb[par][:, s, c * P:(c + 1) * P], ident[:, :])
                        last.then_inc(ctx_turned, 1)

                def project(b):
                    pe.wait_ge(ctx_copied, 2 * b + 2)
                    for k in range(2):
                        for s in range(2):
                            for c in range(KB):
                                last = nc.tensor.matmul(wo_ps[k][:, s * D:(s + 1) * D],
                                                        ctx_t[:, c, (2 * k + s) * P:(2 * k + s + 1) * P],
                                                        wo_cols[:, c, :], start=(c == 0), stop=(c == KB - 1))
                        last.then_inc(wo_done, 1)

                def turn_h1(b, par):
                    pe.wait_ge(h1_ready, b + 1)
                    for c in range(KB):
                        for s in range(SUB):
                            last = nc.tensor.transpose(turn_ps[c][:, s * P:(s + 1) * P],
                                                       h1[par][:, s, c * P:(c + 1) * P], ident[:, :])
                        last.then_inc(h1_turned, 1)

                def up(b, par, first):
                    pe.wait_ge(h1_copied, 2 * b + 2)
                    for m in range(FB):
                        if not (first and m < 2):
                            pe.wait_ge(up_read, FB * b + m - 1)
                        for c in range(KB):
                            last = nc.tensor.matmul(up_ps[m % 2][:, :], w1_cols[:, c, m * P:(m + 1) * P],
                                                    h1_t[par][:, c, :], start=(c == 0), stop=(c == KB - 1))
                        last.then_inc(up_done, 1)

                def down(b, first):
                    pe.wait_ge(up_read, FB * b + FB)
                    for k in range(2):
                        if not first:
                            pe.wait_ge(down_read, 2 * b)
                        for s in range(2):
                            for m in range(FB):
                                last = nc.tensor.matmul(down_ps[k][:, s * D:(s + 1) * D],
                                                        hidden[:, m, (2 * k + s) * P:(2 * k + s + 1) * P],
                                                        w2_cols[:, m, :], start=(m == 0), stop=(m == FB - 1))
                        last.then_inc(down_done, 1)

                turn_pair(wo_rows, 0, turn_ps[0])
                turn_ctx(0, 0, True)
                pe.wait_ge(wt_copied, 1)
                project(0)
                for n, (f0, bank) in enumerate(zip(range(0, FB, 2), other_banks)):
                    turn_pair(w1_rows, f0, bank)
                for n, (m0, bank) in enumerate(zip(range(0, FB, 2), other_banks)):
                    pe.wait_ge(wt_copied, 1 + n + 1)
                    for m in range(2):
                        for f in range(KB):
                            last = nc.tensor.transpose(bank[:, (2 * m + f) * P:(2 * m + f + 1) * P],
                                                       w2_rows[:, f, (m0 + m) * P:(m0 + m + 1) * P], ident[:, :])
                    last.then_inc(wt_turned, 1)
                turn_ctx(1, 1, False)
                project(1)
                turn_h1(0, 0)
                pe.wait_ge(wt_copied, 1 + 2 * len(other_banks))

                def step(b, par, first, last):
                    if not (first or last):
                        turn_ctx(b + 1, 1 - par, False)
                    up(b, par, first)
                    if not (first or last):
                        project(b + 1)
                    down(b, first)
                    if not last:
                        turn_h1(b + 1, 1 - par)

                blockwise(pe, step)

            @block.scalar
            def _(act):
                def copy_pair(n, cols, f0, bank):
                    act.wait_ge(wt_turned, n)
                    nc.scalar.activation(cols[:, :, f0 * P:(f0 + 2) * P],
                                         bank[:, :].rearrange("p (c n) -> p c n", c=KB),
                                         ACT.Copy).then_inc(wt_copied, 1)

                def ctx_copy(b, first):
                    for c in range(KB):
                        act.wait_ge(ctx_turned, 2 * b + c + 1)
                        if not first:
                            act.wait_ge(wo_done, 2 * b)
                        nc.scalar.activation(ctx_t[:, c, :], wo_ps[c][:, :], ACT.Copy).then_inc(ctx_copied, 1)

                def h1_copy(b, par, early):
                    for c in range(KB):
                        act.wait_ge(h1_turned, 2 * b + c + 1)
                        if not early:
                            act.wait_ge(up_done, FB * (b - 1))
                        nc.scalar.activation(h1_t[par][:, c, :], turn_ps[c][:, :], ACT.Copy).then_inc(h1_copied, 1)

                def root(w, before):
                    act.wait_ge(ln_step, before + 11)
                    nc.scalar.activation(std[w][:, :], var_eps[w][:, :], ACT.Sqrt).then_inc(std_ready, 1)

                copy_pair(1, wo_cols, 0, turn_ps[0])
                ctx_copy(0, True)
                act.wait_ge(rows_in, 16 * (len(row_names) + 1))
                for n, bank in enumerate(other_banks):
                    copy_pair(2 + n, w1_cols, 2 * n, bank)
                for n, bank in enumerate(other_banks):
                    act.wait_ge(wt_turned, 2 + len(other_banks) + n)
                    nc.scalar.activation(w2_cols[:, 2 * n:2 * n + 2, :],
                                         bank[:, :].rearrange("p (m n) -> p m n", m=2),
                                         ACT.Copy).then_inc(wt_copied, 1)
                ctx_copy(1, False)
                root(0, 0)
                h1_copy(0, 0, True)

                def step(b, par, first, last):
                    if not (first or last):
                        ctx_copy(b + 1, False)
                    for m in range(FB):
                        if m == 2 and not first:
                            root(1, ln2_before(b - 1, False))
                        act.wait_ge(up_done, FB * b + m + 1)
                        if not first:
                            act.wait_ge(down_done, 2 * b)
                        nc.scalar.activation(hidden[:, m, :], up_ps[m % 2][:, :], ACT.Relu,
                                             bias=b1_cols[:, m:m + 1]).then_inc(up_read, 1)
                    if not last:
                        root(0, ln1_before(b + 1))
                        h1_copy(b + 1, 1 - par, first)

                blockwise(act, step)
                root(1, ln2_before(BLOCKS - 1, True))

            @block.vector
            def _(dve):
                def norm(w, done, which, gain, shift, to, end):
                    for s in range(SUB):
                        nc.vector.bn_stats(stats[w][:, s, :], pre[w][:, s, :]).then_inc(ln_step, 1)
                    dve.wait_ge(ln_step, done + 4)
                    nc.vector.memset(idle[:, :], 0.0)
                    for s in range(SUB):
                        nc.vector.bn_aggr(mean_var[w][:, s, :], stats[w][:, s, :]).then_inc(ln_step, 1)
                    dve.wait_ge(ln_step, done + 8)
                    nc.vector.tensor_scalar(var_eps[w][:, :], mean_var[w][:, :, 1], EPS, None,
                                            ALU.add).then_inc(ln_step, 1)
                    dve.wait_ge(std_ready, which + 1)
                    nc.vector.reciprocal(std_inv[w][:, :], std[w][:, :]).then_inc(ln_step, 1)
                    dve.wait_ge(ln_step, done + 10)
                    nc.vector.tensor_tensor(newton[w][:, :], std_inv[w][:, :], std_inv[w][:, :],
                                            ALU.mult).then_inc(ln_step, 1)
                    dve.wait_ge(ln_step, done + 11)
                    nc.vector.tensor_tensor(newton[w][:, :], newton[w][:, :], var_eps[w][:, :],
                                            ALU.mult).then_inc(ln_step, 1)
                    dve.wait_ge(ln_step, done + 12)
                    nc.vector.tensor_scalar(newton[w][:, :], newton[w][:, :], -0.5, 1.5, ALU.mult,
                                            ALU.add).then_inc(ln_step, 1)
                    dve.wait_ge(ln_step, done + 13)
                    nc.vector.tensor_tensor(std_inv[w][:, :], std_inv[w][:, :], newton[w][:, :],
                                            ALU.mult).then_inc(ln_step, 1)
                    dve.wait_ge(ln_step, done + 14)
                    for s in range(SUB):
                        last = nc.vector.tensor_scalar(to[:, s, :], pre[w][:, s, :], mean_var[w][:, s, 0:1],
                                                       std_inv[w][:, s:s + 1], ALU.subtract, ALU.mult)
                    last.then_inc(ln_step, 1)
                    dve.wait_ge(ln_step, done + 15)
                    for s in range(SUB):
                        last = nc.vector.tensor_tensor(to[:, s, :], to[:, s, :], rows_of[gain][:, :], ALU.mult)
                    last.then_inc(ln_step, 1)
                    dve.wait_ge(ln_step, done + 16)
                    for s in range(SUB):
                        last = nc.vector.tensor_tensor(to[:, s, :], to[:, s, :], rows_of[shift][:, :], ALU.add)
                    last.then_inc(end, 1)

                def ln1(b, par, early):
                    done = 0 if early else ln1_before(b)
                    dve.wait_ge(xr_in[par], 8 * (b - par) + 16)
                    for k in range(2):
                        dve.wait_ge(wo_done, 2 * b + k + 1)
                        for s in range(2):
                            last = nc.vector.tensor_tensor(pre[0][:, 2 * k + s, :], wo_ps[k][:, s * D:(s + 1) * D],
                                                           rows_of["bo"][:, :], ALU.add)
                        last.then_inc(ln_step, 1)
                    dve.wait_ge(ln_step, done + 2)
                    for k in range(2):
                        last = nc.vector.tensor_tensor(pre[0][:, 2 * k:2 * k + 2, :], pre[0][:, 2 * k:2 * k + 2, :],
                                                       x_in_sb[par][:, 2 * k:2 * k + 2, :], ALU.add)
                        last.then_inc(wo_read, 1)
                    dve.wait_ge(wo_read, 2 * b + 2)
                    norm(0, done + 2, 0 if early else 2 * b - 1, "g1", "s1", h1[par], h1_ready)

                def ln2(b, par, early, last_block):
                    done = ln2_before(b, last_block)
                    dve.wait_ge(h1_ready, b + 1)
                    for k in range(2):
                        dve.wait_ge(down_done, 2 * b + k + 1)
                        for s in range(2):
                            last = nc.vector.tensor_tensor(pre[1][:, 2 * k + s, :], down_ps[k][:, s * D:(s + 1) * D],
                                                           rows_of["b2"][:, :], ALU.add)
                        last.then_inc(ln_step, 1)
                    dve.wait_ge(ln_step, done + 2)
                    for k in range(2):
                        last = nc.vector.tensor_tensor(pre[1][:, 2 * k:2 * k + 2, :], pre[1][:, 2 * k:2 * k + 2, :],
                                                       h1[par][:, 2 * k:2 * k + 2, :], ALU.add)
                        last.then_inc(down_read, 1)
                    dve.wait_ge(down_read, 2 * b + 2)
                    if not early:
                        dve.wait_ge(out_stored[par], 8 * (b - par))
                    norm(1, done + 2, 2 * b + (1 if last_block else 2), "g2", "s2", final[par], final_ready)

                dve.wait_ge(rows_in, 16 * (len(row_names) + 1))
                ln1(0, 0, True)

                def step(b, par, first, last):
                    if not first:
                        ln2(b - 1, 1 - par, isinstance(b, int) and b < 3, False)
                    if not last:
                        ln1(b + 1, 1 - par, False)

                blockwise(dve, step)
                ln2(BLOCKS - 1, 1, False, True)


_INS = ["x", "adj", "L0_gnn_Wq", "L0_gnn_bq", "L0_gnn_Wk", "L0_gnn_bk", "L0_gnn_Wv", "L0_gnn_bv", "L0_gnn_Wo",
        "L0_gnn_bo", "L0_gnn_W1", "L0_gnn_b1", "L0_gnn_W2", "L0_gnn_b2", "L0_gnn_ln1_g", "L0_gnn_ln1_b",
        "L0_gnn_ln2_g", "L0_gnn_ln2_b"]


def kernel(**inputs):
    import numpy as _np
    import concourse.bacc as _bacc
    from concourse import mybir as _mybir
    from concourse.bass_utils import run_bass_kernel_spmd as _run

    nc = _bacc.Bacc("TRN2", target_bir_lowering=False, num_devices=1)
    arrays, args = {}, []
    for name in _INS:
        a = _np.ascontiguousarray(inputs[name])
        arrays[f"in_{name}"] = a
        args.append(nc.dram_tensor(f"in_{name}", a.shape, _mybir.dt.from_np(a.dtype), kind="ExternalInput").ap())
    out = nc.dram_tensor("out_h2", inputs["x"].shape, _mybir.dt.float32, kind="ExternalOutput").ap()
    build_gnn_layer(nc, *args, out)
    r = _run(nc, [arrays], core_ids=[0])
    return r.results[0]["out_h2"]
```
